# Optimizing a Trainium2 kernel written in Bass

```python
import numpy as np
import jax
import jax.numpy as jnp

def _softmax(x, axis=-1):
    return jax.nn.softmax(x, axis=axis)

def _gelu(x):
    return jax.nn.gelu(x, approximate=True)

def _silu(x):
    return jax.nn.silu(x)

def _sigmoid(x):
    return jax.nn.sigmoid(x)

def _layernorm(x, axis=-1, eps=1e-05):
    m = jnp.mean(x, axis=axis, keepdims=True)
    v = jnp.var(x, axis=axis, keepdims=True)
    return (x - m) / jnp.sqrt(v + eps)

def _scatter_add(tgt, idx, src, axis=0):
    return tgt.at[idx].add(src)

def _segment_sum(src, seg, n):
    return jax.ops.segment_sum(src, seg, n)
kernel_name = 'mk_xattn_seq_d4_seqx_r4_e0be34'

def setup_inputs(seed: int=0):
    np.random.seed(seed)
    _w = jnp.asarray

    def _rec_inputs():
        import jax
        import jax.numpy as jnp
        _rk = jax.random.key(seed)
        x = -0.0002928 + 1 * jax.random.normal(jax.random.fold_in(_rk, 1), (16, 100, 256), jnp.float32)
        _lenS = 100 - jax.random.randint(jax.random.fold_in(_rk, 7), (16,), 0, max(1, 100 // 4) + 1, jnp.int32)
        _lenS2 = 361 - jax.random.randint(jax.random.fold_in(_rk, 8), (16,), 0, max(1, 361 // 4) + 1, jnp.int32)
        _ctx_1024P = jax.random.normal(jax.random.fold_in(_rk, 11), (16, 16, 256), jnp.float32)
        _ctx_1024c = jax.random.dirichlet(jax.random.fold_in(_rk, 511), 0.3 * jnp.ones((16,), jnp.float32), (16, 361))
        _ctx_1024t = jnp.einsum('bsk,bkd->bsd', _ctx_1024c, _ctx_1024P)
        _ctx_1024t = _ctx_1024t * jax.lax.rsqrt(jnp.mean(jnp.square(_ctx_1024t)) + 1e-12) * 0.953939
        ctx_1024 = -1.39393e-06 + 0.999914 * (_ctx_1024t + 0.3 * jax.random.normal(jax.random.fold_in(_rk, 611), (16, 361, 256), jnp.float32))
        return (x, ctx_1024)
    x, ctx_1024 = _rec_inputs()

    def _L0_xattn_setup():
        import math
        import jax, jax.numpy as jnp
        import numpy as np
        D_MODEL = 256
        EMB = 256
        H = 16
        HD = D_MODEL // H
        B = 2
        S = 512

        def _ln(x, g, b, eps=1e-05):
            m = jnp.mean(x, axis=-1, keepdims=True)
            v = jnp.var(x, axis=-1, keepdims=True)
            return (x - m) * jax.lax.rsqrt(v + eps) * g + b

        def _mha(xq, xk, xv, Wq, bq, Wk, bk, Wv, bv, Wo, bo, causal):
            q = jnp.einsum('bsd,hed->bhse', xq, Wq) + bq[None, :, None, :]
            k = jnp.einsum('bsd,hed->bhse', xk, Wk) + bk[None, :, None, :]
            v = jnp.einsum('bsd,hed->bhse', xv, Wv) + bv[None, :, None, :]
            s = jnp.einsum('bhqe,bhke->bhqk', q, k) * (1.0 / math.sqrt(D_MODEL))
            if causal:
                Lq, Lk = (s.shape[-2], s.shape[-1])
                mask = jnp.tril(jnp.ones((Lq, Lk), dtype=bool))
                s = jnp.where(mask, s, -jnp.inf)
            w = jax.nn.softmax(s, axis=-1)
            o = jnp.einsum('bhqk,bhke->bhqe', w, v)
            b_, h_, s_, e_ = o.shape
            o = o.transpose(0, 2, 1, 3).reshape(b_, s_, h_ * e_)
            return o @ Wo.T + bo

        def _forward(x, encoder_output, sa_q_W, sa_q_b, sa_k_W, sa_k_b, sa_v_W, sa_v_b, ca_q_W, ca_q_b, ca_k_W, ca_k_b, ca_v_W, ca_v_b, m_Wq, m_bq, m_Wk, m_bk, m_Wv, m_bv, m_Wo, m_bo, c_Wq, c_bq, c_Wk, c_bk, c_Wv, c_bv, c_Wo, c_bo, ff_W1, ff_b1, ff_W2, ff_b2, ln1_g, ln1_b, ln2_g, ln2_b, ln3_g, ln3_b):
            q = x @ sa_q_W.T + sa_q_b
            k = x @ sa_k_W.T + sa_k_b
            v = x @ sa_v_W.T + sa_v_b
            sa = _mha(q, k, v, m_Wq, m_bq, m_Wk, m_bk, m_Wv, m_bv, m_Wo, m_bo, causal=True)
            x = _ln(x + sa, ln1_g, ln1_b)
            q = x @ ca_q_W.T + ca_q_b
            k = encoder_output @ ca_k_W.T + ca_k_b
            v = encoder_output @ ca_v_W.T + ca_v_b
            ca = _mha(q, k, v, c_Wq, c_bq, c_Wk, c_bk, c_Wv, c_bv, c_Wo, c_bo, causal=False)
            x = _ln(x + ca, ln2_g, ln2_b)
            h = jax.nn.gelu(x @ ff_W1.T + ff_b1, approximate=False)
            ff = h @ ff_W2.T + ff_b2
            x = _ln(x + ff, ln3_g, ln3_b)
            return x
        key = jax.random.key(seed)
        ks = iter(jax.random.split(key, 64))
        p = lambda *shape: jax.random.normal(next(ks), shape, dtype=jnp.float32) * 0.02
        inp = {'x': jax.random.normal(next(ks), (B, S, EMB), dtype=jnp.float32), 'encoder_output': jax.random.normal(next(ks), (B, S, D_MODEL), dtype=jnp.float32), 'sa_q_W': p(D_MODEL, EMB), 'sa_q_b': p(D_MODEL), 'sa_k_W': p(D_MODEL, EMB), 'sa_k_b': p(D_MODEL), 'sa_v_W': p(D_MODEL, EMB), 'sa_v_b': p(D_MODEL), 'ca_q_W': p(D_MODEL, D_MODEL), 'ca_q_b': p(D_MODEL), 'ca_k_W': p(D_MODEL, D_MODEL), 'ca_k_b': p(D_MODEL), 'ca_v_W': p(D_MODEL, D_MODEL), 'ca_v_b': p(D_MODEL), 'm_Wq': p(H, HD, D_MODEL), 'm_bq': p(H, HD), 'm_Wk': p(H, HD, D_MODEL), 'm_bk': p(H, HD), 'm_Wv': p(H, HD, D_MODEL), 'm_bv': p(H, HD), 'm_Wo': p(D_MODEL, D_MODEL), 'm_bo': p(D_MODEL), 'c_Wq': p(H, HD, D_MODEL), 'c_bq': p(H, HD), 'c_Wk': p(H, HD, D_MODEL), 'c_bk': p(H, HD), 'c_Wv': p(H, HD, D_MODEL), 'c_bv': p(H, HD), 'c_Wo': p(D_MODEL, D_MODEL), 'c_bo': p(D_MODEL), 'ff_W1': p(4 * D_MODEL, D_MODEL), 'ff_b1': p(4 * D_MODEL), 'ff_W2': p(D_MODEL, 4 * D_MODEL), 'ff_b2': p(D_MODEL), 'ln1_g': jnp.ones((D_MODEL,), jnp.float32), 'ln1_b': jnp.zeros((D_MODEL,), jnp.float32), 'ln2_g': jnp.ones((D_MODEL,), jnp.float32), 'ln2_b': jnp.zeros((D_MODEL,), jnp.float32), 'ln3_g': jnp.ones((D_MODEL,), jnp.float32), 'ln3_b': jnp.zeros((D_MODEL,), jnp.float32)}
        return inp
    _L0_xattn_all = _L0_xattn_setup()
    _L0_xattn_in = {k: v for k, v in _L0_xattn_all.items() if k in ('sa_q_W', 'sa_q_b', 'sa_k_W', 'sa_k_b', 'sa_v_W', 'sa_v_b', 'ca_q_W', 'ca_q_b', 'ca_k_W', 'ca_k_b', 'ca_v_W', 'ca_v_b', 'm_Wq', 'm_bq', 'm_Wk', 'm_bk', 'm_Wv', 'm_bv', 'm_Wo', 'm_bo', 'c_Wq', 'c_bq', 'c_Wk', 'c_bk', 'c_Wv', 'c_bv', 'c_Wo', 'c_bo', 'ff_W1', 'ff_b1', 'ff_W2', 'ff_b2', 'ln1_g', 'ln1_b', 'ln2_g', 'ln2_b', 'ln3_g', 'ln3_b')}
    del _L0_xattn_all

    def _L1_xattn_setup():
        import jax, jax.numpy as jnp
        import numpy as np
        MODEL_DIM = 256
        HEAD_SIZE = 64
        N_HEADS = MODEL_DIM // HEAD_SIZE
        HIDDEN = 4 * MODEL_DIM
        B, S = (4, 512)

        def _mha(x, ctx, wq, wk, wv, wo):
            b, s, d = x.shape
            t = ctx.shape[1]
            q = (x @ wq).reshape(b, s, N_HEADS, HEAD_SIZE)
            k = (ctx @ wk).reshape(b, t, N_HEADS, HEAD_SIZE)
            v = (ctx @ wv).reshape(b, t, N_HEADS, HEAD_SIZE)
            scores = jnp.einsum('bqhd,bkhd->bhqk', q, k) / jnp.sqrt(jnp.float32(HEAD_SIZE)).astype(x.dtype)
            attn = jax.nn.softmax(scores, axis=-1)
            out = jnp.einsum('bhqk,bkhd->bqhd', attn, v).reshape(b, s, d)
            return out @ wo

        def _swiglu(x, wg, wu, wd):
            return jax.nn.silu(x @ wg) * (x @ wu) @ wd
        key = jax.random.key(seed)
        ks = jax.random.split(key, 20)
        sc = 0.02
        d, h = (MODEL_DIM, HIDDEN)
        return {'x': jax.random.normal(ks[0], (B, S, d), dtype=jnp.float32), 'y': jax.random.normal(ks[1], (B, S, d), dtype=jnp.float32), 'sa_wq': jax.random.normal(ks[2], (d, d), dtype=jnp.float32) * sc, 'sa_wk': jax.random.normal(ks[3], (d, d), dtype=jnp.float32) * sc, 'sa_wv': jax.random.normal(ks[4], (d, d), dtype=jnp.float32) * sc, 'sa_wo': jax.random.normal(ks[5], (d, d), dtype=jnp.float32) * sc, 'samlp_wg': jax.random.normal(ks[6], (d, h), dtype=jnp.float32) * sc, 'samlp_wu': jax.random.normal(ks[7], (d, h), dtype=jnp.float32) * sc, 'samlp_wd': jax.random.normal(ks[8], (h, d), dtype=jnp.float32) * sc, 'ca_wq': jax.random.normal(ks[9], (d, d), dtype=jnp.float32) * sc, 'ca_wk': jax.random.normal(ks[10], (d, d), dtype=jnp.float32) * sc, 'ca_wv': jax.random.normal(ks[11], (d, d), dtype=jnp.float32) * sc, 'ca_wo': jax.random.normal(ks[12], (d, d), dtype=jnp.float32) * sc, 'camlp_wg': jax.random.normal(ks[13], (d, h), dtype=jnp.float32) * sc, 'camlp_wu': jax.random.normal(ks[14], (d, h), dtype=jnp.float32) * sc, 'camlp_wd': jax.random.normal(ks[15], (h, d), dtype=jnp.float32) * sc}
    _L1_xattn_all = _L1_xattn_setup()
    _L1_xattn_in = {k: v for k, v in _L1_xattn_all.items() if k in ('sa_wq', 'sa_wk', 'sa_wv', 'sa_wo', 'samlp_wg', 'samlp_wu', 'samlp_wd', 'ca_wq', 'ca_wk', 'ca_wv', 'ca_wo', 'camlp_wg', 'camlp_wu', 'camlp_wd')}
    del _L1_xattn_all

    def _L2_xattn_setup():
        import jax, jax.numpy as jnp
        import numpy as np
        EPS = 1e-06

        def _rms(x, scale):
            return x * scale * jax.lax.rsqrt(jnp.mean(x * x, axis=-1, keepdims=True) + EPS)

        def _forward(x, mem_k, mem_v, norm1_scale, norm2_scale, Wq, bq, Wk, bk, Wv, bv, Wz, bz, Wgz, bgz, Wgh, bgh, Wg1, bg1, Wg2, bg2, Wgc1, bgc1, Wgc2, bgc2, Awq, abq, Awk, abk, Awv, abv, Awo, abo, Wf1, bf1, Wf2, bf2):
            B, S, D = x.shape
            M = mem_k.shape[1]
            H = 8
            hd = D // H
            x_norm = _rms(x, norm1_scale)
            q = x_norm @ Wq + bq
            k = x_norm @ Wk + bk
            v = x_norm @ Wv + bv
            z = x_norm @ Wz + bz
            gamma_base = jax.nn.sigmoid(jax.nn.gelu(z @ Wg1 + bg1) @ Wg2 + bg2)
            gamma_mod = jax.nn.sigmoid(jax.nn.gelu(k @ Wgc1 + bgc1) @ Wgc2 + bgc2)
            gamma = jnp.clip(gamma_base * gamma_mod, 1e-06, 1.0 - 1e-06)

            def step(h_prev, zt_gt):
                z_t, g_t = zt_gt
                gate = jax.nn.sigmoid(z_t @ Wgz + bgz + h_prev @ Wgh + bgh)
                h_tilde = (1.0 - gate) * h_prev + gate * z_t
                h_t = h_tilde + g_t * h_prev
                return (h_t, h_t)
            h0 = jnp.zeros((B, D), dtype=x.dtype)
            z_T = jnp.swapaxes(z, 0, 1)
            gamma_T = jnp.swapaxes(gamma, 0, 1)
            _, h_seq_T = jax.lax.scan(step, h0, (z_T, gamma_T))
            h_seq = jnp.swapaxes(h_seq_T, 0, 1)
            qh = (q @ Awq + abq).reshape(B, S, H, hd)
            kh = (mem_k @ Awk + abk).reshape(B, M, H, hd)
            vh = (mem_v @ Awv + abv).reshape(B, M, H, hd)
            scores = jnp.einsum('bshd,bmhd->bhsm', qh, kh) / jnp.sqrt(jnp.asarray(hd, x.dtype))
            probs = jax.nn.softmax(scores, axis=-1)
            mem_out = jnp.einsum('bhsm,bmhd->bshd', probs, vh).reshape(B, S, D) @ Awo + abo
            combined = h_seq + mem_out + v * 0.1
            x_res = x + combined
            x_norm2 = _rms(x_res, norm2_scale)
            ffn = jax.nn.gelu(x_norm2 @ Wf1 + bf1) @ Wf2 + bf2
            return x_res + ffn
        key = jax.random.key(seed)
        B, S, D, H, F, M = (4, 1024, 256, 8, 1024, 128)
        Dq = D // 4
        ks = jax.random.split(key, 24)

        def w(i, shape):
            return jax.random.normal(ks[i], shape, dtype=jnp.float32) * 0.02
        d = {'x': jax.random.normal(ks[0], (B, S, D), dtype=jnp.float32), 'mem_k': jax.random.normal(ks[1], (B, M, D), dtype=jnp.float32), 'mem_v': jax.random.normal(ks[2], (B, M, D), dtype=jnp.float32), 'norm1_scale': jnp.ones((D,), jnp.float32), 'norm2_scale': jnp.ones((D,), jnp.float32), 'Wq': w(3, (D, D)), 'bq': jnp.zeros((D,), jnp.float32), 'Wk': w(4, (D, D)), 'bk': jnp.zeros((D,), jnp.float32), 'Wv': w(5, (D, D)), 'bv': jnp.zeros((D,), jnp.float32), 'Wz': w(6, (D, D)), 'bz': jnp.zeros((D,), jnp.float32), 'Wgz': w(7, (D, D)), 'bgz': jnp.zeros((D,), jnp.float32), 'Wgh': w(8, (D, D)), 'bgh': jnp.zeros((D,), jnp.float32), 'Wg1': w(9, (D, Dq)), 'bg1': jnp.zeros((Dq,), jnp.float32), 'Wg2': w(10, (Dq, D)), 'bg2': jnp.zeros((D,), jnp.float32), 'Wgc1': w(11, (D, Dq)), 'bgc1': jnp.zeros((Dq,), jnp.float32), 'Wgc2': w(12, (Dq, D)), 'bgc2': jnp.zeros((D,), jnp.float32), 'Awq': w(13, (D, D)), 'abq': jnp.zeros((D,), jnp.float32), 'Awk': w(14, (D, D)), 'abk': jnp.zeros((D,), jnp.float32), 'Awv': w(15, (D, D)), 'abv': jnp.zeros((D,), jnp.float32), 'Awo': w(16, (D, D)), 'abo': jnp.zeros((D,), jnp.float32), 'Wf1': w(17, (D, F)), 'bf1': jnp.zeros((F,), jnp.float32), 'Wf2': w(18, (F, D)), 'bf2': jnp.zeros((D,), jnp.float32)}
        return d
    _L2_xattn_all = _L2_xattn_setup()
    _L2_xattn_in = {k: v for k, v in _L2_xattn_all.items() if k in ('norm1_scale', 'norm2_scale', 'Wq', 'bq', 'Wk', 'bk', 'Wv', 'bv', 'Wz', 'bz', 'Wgz', 'bgz', 'Wgh', 'bgh', 'Wg1', 'bg1', 'Wg2', 'bg2', 'Wgc1', 'bgc1', 'Wgc2', 'bgc2', 'Awq', 'abq', 'Awk', 'abk', 'Awv', 'abv', 'Awo', 'abo', 'Wf1', 'bf1', 'Wf2', 'bf2')}
    del _L2_xattn_all

    def _L3_xattn_setup():
        import jax, jax.numpy as jnp
        import numpy as np
        HIDDEN_NUMS = 128
        key = jax.random.key(seed)
        k1, k2, k3 = jax.random.split(key, 3)
        B, S, T, H2 = (32, 256, 64, 2 * HIDDEN_NUMS)
        target_hidden_states = jax.random.normal(k1, (B, T, H2), dtype=jnp.float32)
        hidden_states = jax.random.normal(k2, (B, S, H2), dtype=jnp.float32)
        trans_W = jax.random.uniform(k3, (4 * HIDDEN_NUMS, H2), dtype=jnp.float32, minval=-0.01, maxval=0.01)
        trans_b = jnp.zeros((H2,), dtype=jnp.float32)
        return {'target_hidden_states': target_hidden_states, 'hidden_states': hidden_states, 'trans_W': trans_W, 'trans_b': trans_b}
    _L3_xattn_all = _L3_xattn_setup()
    _L3_xattn_in = {k: v for k, v in _L3_xattn_all.items() if k in ('trans_W', 'trans_b')}
    del _L3_xattn_all
    return {'x': x, 'ctx_1024': ctx_1024, 'L0_xattn_sa_q_W': _L0_xattn_in['sa_q_W'], 'L0_xattn_sa_q_b': _L0_xattn_in['sa_q_b'], 'L0_xattn_sa_k_W': _L0_xattn_in['sa_k_W'], 'L0_xattn_sa_k_b': _L0_xattn_in['sa_k_b'], 'L0_xattn_sa_v_W': _L0_xattn_in['sa_v_W'], 'L0_xattn_sa_v_b': _L0_xattn_in['sa_v_b'], 'L0_xattn_ca_q_W': _L0_xattn_in['ca_q_W'], 'L0_xattn_ca_q_b': _L0_xattn_in['ca_q_b'], 'L0_xattn_ca_k_W': _L0_xattn_in['ca_k_W'], 'L0_xattn_ca_k_b': _L0_xattn_in['ca_k_b'], 'L0_xattn_ca_v_W': _L0_xattn_in['ca_v_W'], 'L0_xattn_ca_v_b': _L0_xattn_in['ca_v_b'], 'L0_xattn_m_Wq': _L0_xattn_in['m_Wq'], 'L0_xattn_m_bq': _L0_xattn_in['m_bq'], 'L0_xattn_m_Wk': _L0_xattn_in['m_Wk'], 'L0_xattn_m_bk': _L0_xattn_in['m_bk'], 'L0_xattn_m_Wv': _L0_xattn_in['m_Wv'], 'L0_xattn_m_bv': _L0_xattn_in['m_bv'], 'L0_xattn_m_Wo': _L0_xattn_in['m_Wo'], 'L0_xattn_m_bo': _L0_xattn_in['m_bo'], 'L0_xattn_c_Wq': _L0_xattn_in['c_Wq'], 'L0_xattn_c_bq': _L0_xattn_in['c_bq'], 'L0_xattn_c_Wk': _L0_xattn_in['c_Wk'], 'L0_xattn_c_bk': _L0_xattn_in['c_bk'], 'L0_xattn_c_Wv': _L0_xattn_in['c_Wv'], 'L0_xattn_c_bv': _L0_xattn_in['c_bv'], 'L0_xattn_c_Wo': _L0_xattn_in['c_Wo'], 'L0_xattn_c_bo': _L0_xattn_in['c_bo'], 'L0_xattn_ff_W1': _L0_xattn_in['ff_W1'], 'L0_xattn_ff_b1': _L0_xattn_in['ff_b1'], 'L0_xattn_ff_W2': _L0_xattn_in['ff_W2'], 'L0_xattn_ff_b2': _L0_xattn_in['ff_b2'], 'L0_xattn_ln1_g': _L0_xattn_in['ln1_g'], 'L0_xattn_ln1_b': _L0_xattn_in['ln1_b'], 'L0_xattn_ln2_g': _L0_xattn_in['ln2_g'], 'L0_xattn_ln2_b': _L0_xattn_in['ln2_b'], 'L0_xattn_ln3_g': _L0_xattn_in['ln3_g'], 'L0_xattn_ln3_b': _L0_xattn_in['ln3_b'], 'L1_xattn_sa_wq': _L1_xattn_in['sa_wq'], 'L1_xattn_sa_wk': _L1_xattn_in['sa_wk'], 'L1_xattn_sa_wv': _L1_xattn_in['sa_wv'], 'L1_xattn_sa_wo': _L1_xattn_in['sa_wo'], 'L1_xattn_samlp_wg': _L1_xattn_in['samlp_wg'], 'L1_xattn_samlp_wu': _L1_xattn_in['samlp_wu'], 'L1_xattn_samlp_wd': _L1_xattn_in['samlp_wd'], 'L1_xattn_ca_wq': _L1_xattn_in['ca_wq'], 'L1_xattn_ca_wk': _L1_xattn_in['ca_wk'], 'L1_xattn_ca_wv': _L1_xattn_in['ca_wv'], 'L1_xattn_ca_wo': _L1_xattn_in['ca_wo'], 'L1_xattn_camlp_wg': _L1_xattn_in['camlp_wg'], 'L1_xattn_camlp_wu': _L1_xattn_in['camlp_wu'], 'L1_xattn_camlp_wd': _L1_xattn_in['camlp_wd'], 'L2_xattn_norm1_scale': _L2_xattn_in['norm1_scale'], 'L2_xattn_norm2_scale': _L2_xattn_in['norm2_scale'], 'L2_xattn_Wq': _L2_xattn_in['Wq'], 'L2_xattn_bq': _L2_xattn_in['bq'], 'L2_xattn_Wk': _L2_xattn_in['Wk'], 'L2_xattn_bk': _L2_xattn_in['bk'], 'L2_xattn_Wv': _L2_xattn_in['Wv'], 'L2_xattn_bv': _L2_xattn_in['bv'], 'L2_xattn_Wz': _L2_xattn_in['Wz'], 'L2_xattn_bz': _L2_xattn_in['bz'], 'L2_xattn_Wgz': _L2_xattn_in['Wgz'], 'L2_xattn_bgz': _L2_xattn_in['bgz'], 'L2_xattn_Wgh': _L2_xattn_in['Wgh'], 'L2_xattn_bgh': _L2_xattn_in['bgh'], 'L2_xattn_Wg1': _L2_xattn_in['Wg1'], 'L2_xattn_bg1': _L2_xattn_in['bg1'], 'L2_xattn_Wg2': _L2_xattn_in['Wg2'], 'L2_xattn_bg2': _L2_xattn_in['bg2'], 'L2_xattn_Wgc1': _L2_xattn_in['Wgc1'], 'L2_xattn_bgc1': _L2_xattn_in['bgc1'], 'L2_xattn_Wgc2': _L2_xattn_in['Wgc2'], 'L2_xattn_bgc2': _L2_xattn_in['bgc2'], 'L2_xattn_Awq': _L2_xattn_in['Awq'], 'L2_xattn_abq': _L2_xattn_in['abq'], 'L2_xattn_Awk': _L2_xattn_in['Awk'], 'L2_xattn_abk': _L2_xattn_in['abk'], 'L2_xattn_Awv': _L2_xattn_in['Awv'], 'L2_xattn_abv': _L2_xattn_in['abv'], 'L2_xattn_Awo': _L2_xattn_in['Awo'], 'L2_xattn_abo': _L2_xattn_in['abo'], 'L2_xattn_Wf1': _L2_xattn_in['Wf1'], 'L2_xattn_bf1': _L2_xattn_in['bf1'], 'L2_xattn_Wf2': _L2_xattn_in['Wf2'], 'L2_xattn_bf2': _L2_xattn_in['bf2'], 'L3_xattn_trans_W': _L3_xattn_in['trans_W'], 'L3_xattn_trans_b': _L3_xattn_in['trans_b']}

def reference(x, ctx_1024, L0_xattn_sa_q_W, L0_xattn_sa_q_b, L0_xattn_sa_k_W, L0_xattn_sa_k_b, L0_xattn_sa_v_W, L0_xattn_sa_v_b, L0_xattn_ca_q_W, L0_xattn_ca_q_b, L0_xattn_ca_k_W, L0_xattn_ca_k_b, L0_xattn_ca_v_W, L0_xattn_ca_v_b, L0_xattn_m_Wq, L0_xattn_m_bq, L0_xattn_m_Wk, L0_xattn_m_bk, L0_xattn_m_Wv, L0_xattn_m_bv, L0_xattn_m_Wo, L0_xattn_m_bo, L0_xattn_c_Wq, L0_xattn_c_bq, L0_xattn_c_Wk, L0_xattn_c_bk, L0_xattn_c_Wv, L0_xattn_c_bv, L0_xattn_c_Wo, L0_xattn_c_bo, L0_xattn_ff_W1, L0_xattn_ff_b1, L0_xattn_ff_W2, L0_xattn_ff_b2, L0_xattn_ln1_g, L0_xattn_ln1_b, L0_xattn_ln2_g, L0_xattn_ln2_b, L0_xattn_ln3_g, L0_xattn_ln3_b, L1_xattn_sa_wq, L1_xattn_sa_wk, L1_xattn_sa_wv, L1_xattn_sa_wo, L1_xattn_samlp_wg, L1_xattn_samlp_wu, L1_xattn_samlp_wd, L1_xattn_ca_wq, L1_xattn_ca_wk, L1_xattn_ca_wv, L1_xattn_ca_wo, L1_xattn_camlp_wg, L1_xattn_camlp_wu, L1_xattn_camlp_wd, L2_xattn_norm1_scale, L2_xattn_norm2_scale, L2_xattn_Wq, L2_xattn_bq, L2_xattn_Wk, L2_xattn_bk, L2_xattn_Wv, L2_xattn_bv, L2_xattn_Wz, L2_xattn_bz, L2_xattn_Wgz, L2_xattn_bgz, L2_xattn_Wgh, L2_xattn_bgh, L2_xattn_Wg1, L2_xattn_bg1, L2_xattn_Wg2, L2_xattn_bg2, L2_xattn_Wgc1, L2_xattn_bgc1, L2_xattn_Wgc2, L2_xattn_bgc2, L2_xattn_Awq, L2_xattn_abq, L2_xattn_Awk, L2_xattn_abk, L2_xattn_Awv, L2_xattn_abv, L2_xattn_Awo, L2_xattn_abo, L2_xattn_Wf1, L2_xattn_bf1, L2_xattn_Wf2, L2_xattn_bf2, L3_xattn_trans_W, L3_xattn_trans_b):
    import jax
    import jax.numpy as jnp

    def _L0_xattn_ref(x, encoder_output, sa_q_W, sa_q_b, sa_k_W, sa_k_b, sa_v_W, sa_v_b, ca_q_W, ca_q_b, ca_k_W, ca_k_b, ca_v_W, ca_v_b, m_Wq, m_bq, m_Wk, m_bk, m_Wv, m_bv, m_Wo, m_bo, c_Wq, c_bq, c_Wk, c_bk, c_Wv, c_bv, c_Wo, c_bo, ff_W1, ff_b1, ff_W2, ff_b2, ln1_g, ln1_b, ln2_g, ln2_b, ln3_g, ln3_b):
        import math
        import jax, jax.numpy as jnp
        import numpy as np
        D_MODEL = 256
        EMB = 256
        H = 16
        HD = D_MODEL // H
        B = 2
        S = 512

        def _ln(x, g, b, eps=1e-05):
            m = jnp.mean(x, axis=-1, keepdims=True)
            v = jnp.var(x, axis=-1, keepdims=True)
            return (x - m) * jax.lax.rsqrt(v + eps) * g + b

        def _mha(xq, xk, xv, Wq, bq, Wk, bk, Wv, bv, Wo, bo, causal):
            q = jnp.einsum('bsd,hed->bhse', xq, Wq) + bq[None, :, None, :]
            k = jnp.einsum('bsd,hed->bhse', xk, Wk) + bk[None, :, None, :]
            v = jnp.einsum('bsd,hed->bhse', xv, Wv) + bv[None, :, None, :]
            s = jnp.einsum('bhqe,bhke->bhqk', q, k) * (1.0 / math.sqrt(D_MODEL))
            if causal:
                Lq, Lk = (s.shape[-2], s.shape[-1])
                mask = jnp.tril(jnp.ones((Lq, Lk), dtype=bool))
                s = jnp.where(mask, s, -jnp.inf)
            w = jax.nn.softmax(s, axis=-1)
            o = jnp.einsum('bhqk,bhke->bhqe', w, v)
            b_, h_, s_, e_ = o.shape
            o = o.transpose(0, 2, 1, 3).reshape(b_, s_, h_ * e_)
            return o @ Wo.T + bo

        def _forward(x, encoder_output, sa_q_W, sa_q_b, sa_k_W, sa_k_b, sa_v_W, sa_v_b, ca_q_W, ca_q_b, ca_k_W, ca_k_b, ca_v_W, ca_v_b, m_Wq, m_bq, m_Wk, m_bk, m_Wv, m_bv, m_Wo, m_bo, c_Wq, c_bq, c_Wk, c_bk, c_Wv, c_bv, c_Wo, c_bo, ff_W1, ff_b1, ff_W2, ff_b2, ln1_g, ln1_b, ln2_g, ln2_b, ln3_g, ln3_b):
            q = x @ sa_q_W.T + sa_q_b
            k = x @ sa_k_W.T + sa_k_b
            v = x @ sa_v_W.T + sa_v_b
            sa = _mha(q, k, v, m_Wq, m_bq, m_Wk, m_bk, m_Wv, m_bv, m_Wo, m_bo, causal=True)
            x = _ln(x + sa, ln1_g, ln1_b)
            q = x @ ca_q_W.T + ca_q_b
            k = encoder_output @ ca_k_W.T + ca_k_b
            v = encoder_output @ ca_v_W.T + ca_v_b
            ca = _mha(q, k, v, c_Wq, c_bq, c_Wk, c_bk, c_Wv, c_bv, c_Wo, c_bo, causal=False)
            x = _ln(x + ca, ln2_g, ln2_b)
            h = jax.nn.gelu(x @ ff_W1.T + ff_b1, approximate=False)
            ff = h @ ff_W2.T + ff_b2
            x = _ln(x + ff, ln3_g, ln3_b)
            return x
        return _forward(x, encoder_output, sa_q_W, sa_q_b, sa_k_W, sa_k_b, sa_v_W, sa_v_b, ca_q_W, ca_q_b, ca_k_W, ca_k_b, ca_v_W, ca_v_b, m_Wq, m_bq, m_Wk, m_bk, m_Wv, m_bv, m_Wo, m_bo, c_Wq, c_bq, c_Wk, c_bk, c_Wv, c_bv, c_Wo, c_bo, ff_W1, ff_b1, ff_W2, ff_b2, ln1_g, ln1_b, ln2_g, ln2_b, ln3_g, ln3_b)

    def _L1_xattn_ref(x, y, sa_wq, sa_wk, sa_wv, sa_wo, samlp_wg, samlp_wu, samlp_wd, ca_wq, ca_wk, ca_wv, ca_wo, camlp_wg, camlp_wu, camlp_wd):
        import jax, jax.numpy as jnp
        import numpy as np
        MODEL_DIM = 256
        HEAD_SIZE = 64
        N_HEADS = MODEL_DIM // HEAD_SIZE
        HIDDEN = 4 * MODEL_DIM
        B, S = (4, 512)

        def _mha(x, ctx, wq, wk, wv, wo):
            b, s, d = x.shape
            t = ctx.shape[1]
            q = (x @ wq).reshape(b, s, N_HEADS, HEAD_SIZE)
            k = (ctx @ wk).reshape(b, t, N_HEADS, HEAD_SIZE)
            v = (ctx @ wv).reshape(b, t, N_HEADS, HEAD_SIZE)
            scores = jnp.einsum('bqhd,bkhd->bhqk', q, k) / jnp.sqrt(jnp.float32(HEAD_SIZE)).astype(x.dtype)
            attn = jax.nn.softmax(scores, axis=-1)
            out = jnp.einsum('bhqk,bkhd->bqhd', attn, v).reshape(b, s, d)
            return out @ wo

        def _swiglu(x, wg, wu, wd):
            return jax.nn.silu(x @ wg) * (x @ wu) @ wd
        x = x + _mha(x, x, sa_wq, sa_wk, sa_wv, sa_wo)
        x = x + _swiglu(x, samlp_wg, samlp_wu, samlp_wd)
        x = x + _mha(x, y, ca_wq, ca_wk, ca_wv, ca_wo)
        x = x + _swiglu(x, camlp_wg, camlp_wu, camlp_wd)
        return x

    def _L2_xattn_ref(x, mem_k, mem_v, norm1_scale, norm2_scale, Wq, bq, Wk, bk, Wv, bv, Wz, bz, Wgz, bgz, Wgh, bgh, Wg1, bg1, Wg2, bg2, Wgc1, bgc1, Wgc2, bgc2, Awq, abq, Awk, abk, Awv, abv, Awo, abo, Wf1, bf1, Wf2, bf2):
        import jax, jax.numpy as jnp
        import numpy as np
        EPS = 1e-06

        def _rms(x, scale):
            return x * scale * jax.lax.rsqrt(jnp.mean(x * x, axis=-1, keepdims=True) + EPS)

        def _forward(x, mem_k, mem_v, norm1_scale, norm2_scale, Wq, bq, Wk, bk, Wv, bv, Wz, bz, Wgz, bgz, Wgh, bgh, Wg1, bg1, Wg2, bg2, Wgc1, bgc1, Wgc2, bgc2, Awq, abq, Awk, abk, Awv, abv, Awo, abo, Wf1, bf1, Wf2, bf2):
            B, S, D = x.shape
            M = mem_k.shape[1]
            H = 8
            hd = D // H
            x_norm = _rms(x, norm1_scale)
            q = x_norm @ Wq + bq
            k = x_norm @ Wk + bk
            v = x_norm @ Wv + bv
            z = x_norm @ Wz + bz
            gamma_base = jax.nn.sigmoid(jax.nn.gelu(z @ Wg1 + bg1) @ Wg2 + bg2)
            gamma_mod = jax.nn.sigmoid(jax.nn.gelu(k @ Wgc1 + bgc1) @ Wgc2 + bgc2)
            gamma = jnp.clip(gamma_base * gamma_mod, 1e-06, 1.0 - 1e-06)

            def step(h_prev, zt_gt):
                z_t, g_t = zt_gt
                gate = jax.nn.sigmoid(z_t @ Wgz + bgz + h_prev @ Wgh + bgh)
                h_tilde = (1.0 - gate) * h_prev + gate * z_t
                h_t = h_tilde + g_t * h_prev
                return (h_t, h_t)
            h0 = jnp.zeros((B, D), dtype=x.dtype)
            z_T = jnp.swapaxes(z, 0, 1)
            gamma_T = jnp.swapaxes(gamma, 0, 1)
            _, h_seq_T = jax.lax.scan(step, h0, (z_T, gamma_T))
            h_seq = jnp.swapaxes(h_seq_T, 0, 1)
            qh = (q @ Awq + abq).reshape(B, S, H, hd)
            kh = (mem_k @ Awk + abk).reshape(B, M, H, hd)
            vh = (mem_v @ Awv + abv).reshape(B, M, H, hd)
            scores = jnp.einsum('bshd,bmhd->bhsm', qh, kh) / jnp.sqrt(jnp.asarray(hd, x.dtype))
            probs = jax.nn.softmax(scores, axis=-1)
            mem_out = jnp.einsum('bhsm,bmhd->bshd', probs, vh).reshape(B, S, D) @ Awo + abo
            combined = h_seq + mem_out + v * 0.1
            x_res = x + combined
            x_norm2 = _rms(x_res, norm2_scale)
            ffn = jax.nn.gelu(x_norm2 @ Wf1 + bf1) @ Wf2 + bf2
            return x_res + ffn
        return _forward(x, mem_k, mem_v, norm1_scale, norm2_scale, Wq, bq, Wk, bk, Wv, bv, Wz, bz, Wgz, bgz, Wgh, bgh, Wg1, bg1, Wg2, bg2, Wgc1, bgc1, Wgc2, bgc2, Awq, abq, Awk, abk, Awv, abv, Awo, abo, Wf1, bf1, Wf2, bf2)

    def _L3_xattn_ref(target_hidden_states, hidden_states, trans_W, trans_b):
        import jax, jax.numpy as jnp
        import numpy as np
        HIDDEN_NUMS = 128
        scores = jnp.einsum('bsd,btd->bst', hidden_states, target_hidden_states)
        attn = jax.nn.softmax(scores, axis=-1)
        ti = jnp.einsum('bst,btd->bsd', attn, target_hidden_states)
        cat = jnp.concatenate([hidden_states, ti], axis=-1)
        hi_new = jnp.tanh(jnp.einsum('bsf,fd->bsd', cat, trans_W) + trans_b)
        return hi_new + hidden_states
    x = _L0_xattn_ref(x, ctx_1024, L0_xattn_sa_q_W, L0_xattn_sa_q_b, L0_xattn_sa_k_W, L0_xattn_sa_k_b, L0_xattn_sa_v_W, L0_xattn_sa_v_b, L0_xattn_ca_q_W, L0_xattn_ca_q_b, L0_xattn_ca_k_W, L0_xattn_ca_k_b, L0_xattn_ca_v_W, L0_xattn_ca_v_b, L0_xattn_m_Wq, L0_xattn_m_bq, L0_xattn_m_Wk, L0_xattn_m_bk, L0_xattn_m_Wv, L0_xattn_m_bv, L0_xattn_m_Wo, L0_xattn_m_bo, L0_xattn_c_Wq, L0_xattn_c_bq, L0_xattn_c_Wk, L0_xattn_c_bk, L0_xattn_c_Wv, L0_xattn_c_bv, L0_xattn_c_Wo, L0_xattn_c_bo, L0_xattn_ff_W1, L0_xattn_ff_b1, L0_xattn_ff_W2, L0_xattn_ff_b2, L0_xattn_ln1_g, L0_xattn_ln1_b, L0_xattn_ln2_g, L0_xattn_ln2_b, L0_xattn_ln3_g, L0_xattn_ln3_b)
    x = _L1_xattn_ref(x, ctx_1024, L1_xattn_sa_wq, L1_xattn_sa_wk, L1_xattn_sa_wv, L1_xattn_sa_wo, L1_xattn_samlp_wg, L1_xattn_samlp_wu, L1_xattn_samlp_wd, L1_xattn_ca_wq, L1_xattn_ca_wk, L1_xattn_ca_wv, L1_xattn_ca_wo, L1_xattn_camlp_wg, L1_xattn_camlp_wu, L1_xattn_camlp_wd)
    x = _L2_xattn_ref(x, ctx_1024, ctx_1024, L2_xattn_norm1_scale, L2_xattn_norm2_scale, L2_xattn_Wq, L2_xattn_bq, L2_xattn_Wk, L2_xattn_bk, L2_xattn_Wv, L2_xattn_bv, L2_xattn_Wz, L2_xattn_bz, L2_xattn_Wgz, L2_xattn_bgz, L2_xattn_Wgh, L2_xattn_bgh, L2_xattn_Wg1, L2_xattn_bg1, L2_xattn_Wg2, L2_xattn_bg2, L2_xattn_Wgc1, L2_xattn_bgc1, L2_xattn_Wgc2, L2_xattn_bgc2, L2_xattn_Awq, L2_xattn_abq, L2_xattn_Awk, L2_xattn_abk, L2_xattn_Awv, L2_xattn_abv, L2_xattn_Awo, L2_xattn_abo, L2_xattn_Wf1, L2_xattn_bf1, L2_xattn_Wf2, L2_xattn_bf2)
    x = _L3_xattn_ref(ctx_1024, x, L3_xattn_trans_W, L3_xattn_trans_b)
    return x

_drawn_inputs = setup_inputs


def setup_inputs(seed=0):
    import zlib

    import numpy as np

    out = dict(_drawn_inputs(seed))
    spreads = {'L0_xattn_ln1_g': (1.0, 0.2),
     'L0_xattn_ln1_b': (0.0, 0.1),
     'L0_xattn_ln2_g': (1.0, 0.2),
     'L0_xattn_ln2_b': (0.0, 0.1),
     'L0_xattn_ln3_g': (1.0, 0.2),
     'L0_xattn_ln3_b': (0.0, 0.1),
     'L2_xattn_norm1_scale': (1.0, 0.2),
     'L2_xattn_norm2_scale': (1.0, 0.2),
     'L2_xattn_bq': (0.0, 0.1),
     'L2_xattn_bk': (0.0, 0.1),
     'L2_xattn_bv': (0.0, 0.1),
     'L2_xattn_bz': (0.0, 0.1),
     'L2_xattn_bgz': (0.0, 0.1),
     'L2_xattn_bgh': (0.0, 0.1),
     'L2_xattn_bg1': (0.0, 0.1),
     'L2_xattn_bg2': (0.0, 0.1),
     'L2_xattn_bgc1': (0.0, 0.1),
     'L2_xattn_bgc2': (0.0, 0.1),
     'L2_xattn_abq': (0.0, 0.1),
     'L2_xattn_abk': (0.0, 0.1),
     'L2_xattn_abv': (0.0, 0.1),
     'L2_xattn_abo': (0.0, 0.1),
     'L2_xattn_bf1': (0.0, 0.1),
     'L2_xattn_bf2': (0.0, 0.1),
     'L3_xattn_trans_b': (0.0, 0.1)}
    factors = {}
    for name, (base, spread) in spreads.items():
        noise = np.random.default_rng([zlib.crc32(name.encode()), seed]).standard_normal(out[name].shape)
        drawn = base * np.exp(spread * noise) if base else spread * noise
        out[name] = jnp.asarray(drawn.astype(out[name].dtype))
    for name, factor in factors.items():
        out[name] = (out[name] * factor).astype(out[name].dtype)
    return out
```

```python
import math
from contextlib import ExitStack

import concourse.bass as bass
import numpy as np
from concourse import mybir

F32 = mybir.dt.float32
F32R = mybir.dt.float32r
BF16 = mybir.dt.bfloat16
ACT = mybir.ActivationFunctionType
ALU = mybir.AluOpType
AX = mybir.AxisListType.X

B, S, C, D, FF = 16, 100, 361, 256, 1024
P = 128
DC = D // P
GB = 4
NG = B // GB
N = GB * S
KCH = [(0, 128), (128, 128), (256, C - 256)]
SCH = [(0, S)]
MASKED = -1.0e30

FOLDS = [("sq", "sa_q_b", "m_bq"), ("sk", "sa_k_b", "m_bk"), ("sv", "sa_v_b", "m_bv"),
         ("cq", "ca_q_b", "c_bq"), ("ck", "ca_k_b", "c_bk"), ("cv", "ca_v_b", "c_bv"), ("q2", "bq", "abq")]

VECS = [(n, DC) for n in ("sa_q_b", "sa_k_b", "sa_v_b", "ca_q_b", "ca_k_b", "ca_v_b",
                          "m_bq", "m_bk", "m_bv", "m_bo", "c_bq", "c_bk", "c_bv", "c_bo", "ff_b2",
                          "ln1_g", "ln1_b", "ln2_g", "ln2_b", "ln3_g", "ln3_b",
                          "norm1", "norm2", "bq", "bk", "bv", "bz", "bgz", "bgh", "bg2", "bgc2",
                          "abq", "abk", "abv", "abo", "bf2", "trans_b")]
VECS += [("ff_b1", FF // P), ("bf1", FF // P), ("bg1", 1), ("bgc1", 1)]
DERIVED = [(n, DC) for n in ("d_sq", "d_sk", "d_sv", "d_so", "d_cq", "d_ck", "d_cv", "d_co", "d_q2", "d_gz", "d_o2")]
DERIVED += [("d_k2", 1)]


def offsets(parts):
    at, out = 0, {}
    for name, size in parts:
        out[name] = at
        at += size
    return out, at


VAT, NVEC = offsets(VECS + DERIVED)
NVEC_IN = sum(s for _, s in VECS)
SQ = DC * D
W0 = [("so", SQ), ("co", SQ), ("ff1", DC * FF), ("ff2", FF // P * D)]
W0F = [("sq", SQ), ("sk", SQ), ("sv", SQ), ("cq", SQ), ("ck", SQ), ("cv", SQ), ("q2", SQ), ("k2", DC * 64)]
W1 = [("l1_sq", SQ), ("l1_sk", SQ), ("l1_sv", SQ), ("l1_so", SQ), ("g1", DC * FF), ("u1", DC * FF), ("d1", FF // P * D),
      ("l1_cq", SQ), ("l1_ck", SQ), ("l1_cv", SQ), ("l1_co", SQ), ("g2", DC * FF), ("u2", DC * FF), ("d2", FF // P * D)]
W2 = [("z", SQ), ("gz", SQ), ("v2", SQ), ("awk", SQ), ("awv", SQ), ("awo", SQ), ("wg1", DC * 64), ("wg2", D), ("gc2", D)]
WAT, NW = offsets(W0F + W0 + W1 + W2)
NWF = sum(s for _, s in W0F)
NW0, NW1, NW2 = (sum(s for _, s in w) for w in (W0, W1, W2))
FOLD_SRC = 2 * SQ
NSRC = len(FOLDS) * FOLD_SRC + SQ + DC * 64
T_W = [("wgh", SQ), ("f1", DC * FF), ("f2", FF // P * D), ("trans", 2 * SQ)]
NTW = sum(s for _, s in T_W)
TAT, NT = offsets(T_W + [("zs", DC * B * S), ("gzs", DC * B * S), ("gms", DC * B * S), ("base", DC * B * S), ("hs", DC * B * S)])
assert NT <= NW
CONSTS = [("ident", P), ("negid", P), ("neg", S), ("negT", S), ("hm16", 8), ("hm64", 2), ("hm32", 4), ("em4", 4), ("em2", 2)]
CAT, NCONST = offsets(CONSTS)


def constants():
    c = np.zeros((P, NCONST), np.float32)
    p = np.arange(P)
    c[p, CAT["ident"] + p] = 1.0
    c[p, CAT["negid"] + p] = -1.0
    q = np.arange(S)
    c[:S, CAT["neg"]:CAT["neg"] + S] = np.where(q[:, None] >= q[None, :], 0.0, MASKED)
    c[:S, CAT["negT"]:CAT["negT"] + S] = np.where(q[None, :] >= q[:, None], 0.0, MASKED)
    for name, rows in (("hm16", 16), ("hm64", 64), ("hm32", 32)):
        c[p, CAT[name] + p // rows] = 1.0
    c[p, CAT["em4"] + p % 64 // 16] = 1.0
    c[p, CAT["em2"] + p % 64 // 32] = 1.0
    return c


class Book:

    def __init__(self, known=None):
        self.marks = {}
        self.totals = {}
        self.banks = {}
        self.known = known


PHASES = [("prepare", 1), ("group", NG), ("load", 1), ("scan", S // 2), ("tail", NG)]


def build(nc, book, x_in, ctx_in, vec_in, const_in, src_in, w0_in, w1_in, w2_in, tw_in, out, spill):
    known = book.known
    with ExitStack() as ctx:
        def sb(name, shape, dt=F32):
            return ctx.enter_context(nc.sbuf_tensor(name, shape, dt))

        WT = sb("weights", [P, NW])
        X = sb("x_resid", [P, DC, N])
        T1 = sb("t1", [P, DC, N])
        T2 = sb("t2", [P, DC, N])
        QO = sb("q_then_o", [P, DC, N])
        K2 = sb("k_self", [P, DC, N])
        CT = sb("ctx_t", [P, GB, DC, C])
        KC = sb("k_ctx", [P, 2, DC, C])
        VA = sb("v_and_ones", [P, 2, 3, DC, 4, 64])
        PQ = sb("probs_and_q", [P, 4800 + 3200])
        MD = sb("max_diag", [S, 16, S], F32R)
        CST = sb("ctx_stage", [P, 3, D])
        EX = sb("extract", [P, 4, S])
        EM = sb("extract_m", [P, 4 * S])
        DN = sb("denoms", [P, DC, S])
        MX = sb("maxima", [S, 2, 16])
        VEC = sb("vectors", [P, NVEC])
        CO = sb("constants", [P, NCONST])
        ONEM = sb("ones_mean", [P, P])
        ONER = sb("ones_r", [S, P], F32R)
        IDB = sb("ident_bf", [S, S], BF16)
        NEGB = sb("neg_bf", [S, 4, S], BF16)
        NEGTB = sb("negT_bf", [S, 4, S], BF16)
        EPS = sb("eps", [P, 2])
        PS = ctx.enter_context(nc.psum_tensor("psum", [P, 8, 512], F32))

        state = [EM[:, i * DC * B:(i + 1) * DC * B].rearrange("p (c b) -> p c b", c=DC) for i in range(4)]
        GA, ZH, HG, GU = state
        HC = EX[:, 0, 0:2 * DC * B].rearrange("p (a c b) -> p a c b", a=2, c=DC)

        PT = PQ[:, 0:4800].rearrange("p (c n) -> p c n", c=3)
        PF = PQ[:, 0:4800]
        QB = PQ[:, 4800:8000].rearrange("p (a c n) -> p a c n", a=2, c=DC)
        XST = PQ[:, 0:GB * D].rearrange("p (b d) -> p b d", b=GB)
        H = PQ[:, 0:3200].rearrange("p (m n) -> p m n", m=8)
        U = PQ[:, 3200:4000].rearrange("p (m n) -> p m n", m=2)
        GZ = PF[:, 0:800].rearrange("p (m n) -> p m n", m=2)
        GM = PF[:, 800:1600].rearrange("p (m n) -> p m n", m=2)
        GH = PF[:, 1600:2400].rearrange("p (m n) -> p m n", m=2)
        SG = PF[:, 2400:3200].rearrange("p (m n) -> p m n", m=2)
        YO = PF[:, 1600:1600 + GB * D].rearrange("p (b d) -> p b d", b=GB)
        PL3 = PF[:, 2700:2700 + C]

        def w(name, k, m0, m1, width=D, rows=P):
            o = WAT[name] + k * width
            return WT[0:rows, o + m0:o + m1]

        def tw(name, k, m0, m1, width=D):
            o = TAT[name] + k * width
            return WT[:, o + m0:o + m1]

        def vec(name, m=0, rows=P):
            return VEC[0:rows, VAT[name] + m:VAT[name] + m + 1]

        def const(name, size, rows=P):
            return CO[0:rows, CAT[name]:CAT[name] + size]

        IDENT = const("ident", P)
        seq = lambda name: WT[:, TAT[name]:TAT[name] + DC * B * S]

        def sem(name):
            return ctx.enter_context(nc.semaphore(name))

        products_ready, act_results, dve_results, pool_results = (
            sem(n) for n in ("products_ready", "act_results", "dve_results", "pool_results"))
        x_loaded, ctx_loaded, weights_loaded, weights1_loaded, fold_sources_loaded = (
            sem(n) for n in ("x_loaded", "ctx_loaded", "weights_loaded", "weights1_loaded", "fold_sources_loaded"))
        constants_loaded, spilled, sequences_loaded, outputs_stored = (
            sem(n) for n in ("constants_loaded", "spilled", "sequences_loaded", "outputs_stored"))
        sems = {"pe": products_ready, "act": act_results, "dve": dve_results, "pool": pool_results, "x": x_loaded,
                "ctx": ctx_loaded, "w": weights_loaded, "w1": weights1_loaded, "src": fold_sources_loaded,
                "cst": constants_loaded, "spill": spilled, "seq": sequences_loaded, "out": outputs_stored}
        counts = dict.fromkeys(sems, 0)
        phase = {"name": None, "it": 0}
        waited = {}

        def before(track):
            total = 0
            for name, times in PHASES:
                per = known.totals.get((name, track), 0) if known else 0
                if name == phase["name"]:
                    return total, per
                total += per * times
            raise KeyError(phase["name"])

        def mark(track, point, by=1):
            counts[track] += by
            book.marks[phase["name"], point] = (track, counts[track])
            book.totals[phase["name"], track] = counts[track]
            return by

        def at(point):
            if not known:
                return 0
            track, n = known.marks[phase["name"], point]
            base, per = before(track)
            return phase["it"] * per + (base + n) if phase["loop"] else base + n

        def due(point):
            if not known:
                return True
            track, n = known.marks[phase["name"], point]
            if waited.get(track, 0) >= n:
                return False
            waited[track] = n
            return True

        def producer(point):
            return sems[known.marks[phase["name"], point][0]] if known else products_ready

        def enter(eng, name, it, of=None):
            phase.update(name=name, it=it, loop=dict(PHASES)[name] > 1)
            counts.update(dict.fromkeys(sems, 0))
            waited.clear()
            for track in (of or sems) if known else ():
                base, per = before(track)
                if phase["loop"] and per:
                    eng.wait_ge(sems[track], it * per + base)
                elif base:
                    eng.wait_ge(sems[track], base)

        def bank(use):
            return known.banks[phase["name"], use] if known else 0

        class Ring:

            def __init__(self, banks):
                self.banks = banks

            def start(self):
                self.k, self.freed = 0, {}

            def take(self, pe, use, freed_by):
                b = self.banks[self.k % len(self.banks)]
                self.k += 1
                if b in self.freed:
                    if due(self.freed[b]):
                        pe.wait_ge(producer(self.freed[b]), at(self.freed[b]))
                self.freed[b] = freed_by
                book.banks[phase["name"], use] = b
                return b

        rings = {"lin": Ring([0, 1]), "max": Ring([2, 3]), "st": Ring([4, 5]), "pv": Ring([6, 7])}

        def rings_start():
            for r in rings.values():
                r.start()

        ATT = {
            "s0": dict(heads=16, self=True, causal=True, mask="hm16", em="em4"),
            "c0": dict(heads=16, self=False, causal=False, mask="hm16", em="em4"),
            "s1": dict(heads=4, self=True, causal=False, mask="hm64", em=None),
            "c1": dict(heads=4, self=False, causal=False, mask="hm64", em=None),
            "c2": dict(heads=8, self=False, causal=False, mask="hm32", em="em2"),
        }
        for a in ATT.values():
            a["hc"] = a["heads"] // DC
            a["hg"] = a["heads"] // 4
            a["keys"] = SCH if a["self"] else KCH
            a["nk"] = S if a["self"] else C
        WN = {"s0": ("sq", "sk", "sv"), "c0": ("cq", "ck", "cv"), "s1": ("l1_sq", "l1_sk", "l1_sv"),
              "c1": ("l1_cq", "l1_ck", "l1_cv"), "c2": ("q2", "awk", "awv")}
        QSC = {"s0": 1 / 16, "c0": 1 / 16, "s1": 1 / 8, "c1": 1 / 8, "c2": 1 / math.sqrt(32)}
        QBIAS = {"s0": "d_sq", "c0": "d_cq", "c2": "d_q2"}
        KBIAS = {"s0": "d_sk", "c0": "d_ck", "c2": "abk"}

        def keys_of(t, b, c, k0, kn):
            return K2[:, c, b * S + k0:b * S + k0 + kn] if ATT[t]["self"] else KC[:, b % 2, c, k0:k0 + kn]

        def qblock(b, c, h0, nh, hc):
            return QB[:, b % 2, c, h0 * S:(h0 + nh) * S]

        def pe_linear(pe, use, lhs, rhs, n, ms=DC, rows=P, ring="lin"):
            for m in range(ms):
                bk = rings[ring].take(pe, f"{use}{m}", f"{use}{m} out")
                for k, r in enumerate(rhs):
                    i = nc.tensor.matmul(PS[0:rows, bk, 0:n], lhs(k, m), r, start=k == 0, stop=k == len(rhs) - 1)
                i.then_inc(products_ready, mark("pe", f"{use}{m}"))

        def sq(name, rows=P):
            return lambda k, m: w(name, k, m * P, (m + 1) * P)

        def chunks(t):
            return [t[:, c, :] for c in range(DC)]

        def pe_kv(pe, t, b):
            a = ATT[t]
            _, wk, wv = WN[t]
            if not a["self"]:
                pe_linear(pe, f"{t} k{b} ", sq(wk), [CT[:, b, c, :] for c in range(DC)], C)
            src = {"s0": X, "s1": X}.get(t)
            for kc, (k0, kn) in enumerate(a["keys"]):
                bk = rings["lin"].take(pe, f"{t} v{b} {kc}", f"{t} v{b} {kc} out")
                for c in range(DC):
                    lhs = src[:, c, b * S:(b + 1) * S] if a["self"] else CT[:, b, c, k0:k0 + kn]
                    i = nc.tensor.matmul(PS[0:kn, bk, 0:D], lhs, w(wv, c, 0, D), start=c == 0, stop=c == DC - 1)
                i.then_inc(products_ready, mark("pe", f"{t} v{b} {kc}"))

        def pe_max(pe, t, b):
            a = ATT[t]
            if due(f"{t} qb{b} 1"):
                pe.wait_ge(pool_results, at(f"{t} qb{b} 1"))
            if not a["self"]:
                if due(f"{t} k{b} 1 out"):
                    pe.wait_ge(act_results, at(f"{t} k{b} 1 out"))
            if a["self"]:
                for u in range(a["heads"] // 4):
                    bk = rings["max"].take(pe, f"{t} s{b} {u}", f"{t} m{b} {u}")
                    for j in range(4):
                        if a["causal"]:
                            nc.tensor.matmul(PS[0:S, bk, j * S:(j + 1) * S], IDB[:, :], NEGB[:, j, :], start=True, stop=False)
                        h = 4 * u + j
                        c, hh = divmod(h, a["hc"])
                        i = nc.tensor.matmul(PS[0:S, bk, j * S:(j + 1) * S], qblock(b, c, hh, 1, a["hc"]), keys_of(t, b, c, 0, S),
                                             start=not a["causal"], stop=True)
                    i.then_inc(products_ready, mark("pe", f"{t} s{b} {u}"))
                return
            for h in range(a["heads"]):
                c, hh = divmod(h, a["hc"])
                bk = rings["max"].take(pe, f"{t} s{b} {h}", f"{t} m{b} {h}")
                nc.tensor.matmul(PS[0:S, bk, 0:C], qblock(b, c, hh, 1, a["hc"]), keys_of(t, b, c, 0, C), start=True, stop=True).then_inc(products_ready, mark("pe", f"{t} s{b} {h}"))

        def pe_scores(pe, t, b):
            a = ATT[t]
            if due(f"{t} md{b}"):
                pe.wait_ge(dve_results, at(f"{t} md{b}"))
            for kc, (k0, kn) in enumerate(a["keys"]):
                for u in range(a["heads"] // 4):
                    bk = rings["st"].take(pe, f"{t} st{b} {kc} {u}", f"{t} p{b} {kc} {u}")
                    o = PS[0:kn, bk, :]
                    nh = min(4, a["hc"])
                    for j in range(0, 4, nh):
                        nc.tensor.matmul(o[:, j * S:(j + nh) * S], ONER[:, 0:kn], MD[:, 4 * u + j:4 * u + j + nh, :], start=True, stop=False)
                        if a["causal"]:
                            nc.tensor.matmul(o[:, 0:N], IDB[:, :], NEGTB[:, :, :], start=False, stop=False)
                        c, hh = divmod(4 * u + j, a["hc"])
                        i = nc.tensor.matmul(o[:, j * S:(j + nh) * S], keys_of(t, b, c, k0, kn), qblock(b, c, hh, nh, a["hc"]),
                                             start=False, stop=True)
                    i.then_inc(products_ready, mark("pe", f"{t} st{b} {kc} {u}"))

        def pe_values(pe, t, b):
            a = ATT[t]
            hg = a["hg"]
            last = len(a["keys"]) - 1
            for kc in range(last + 1):
                if due(f"{t} v{b} {kc} out"):
                    pe.wait_ge(act_results, at(f"{t} v{b} {kc} out"))
            for g in range(4):
                bk = rings["pv"].take(pe, f"{t} o{b} {g}", f"{t} e{b} {g}")
                if due(f"{t} p{b} {last} {(g * hg + hg - 1) // 4}"):
                    pe.wait_ge(act_results, at(f"{t} p{b} {last} {(g * hg + hg - 1) // 4}"))
                for kc, (k0, kn) in enumerate(a["keys"]):
                    v = VA[0:kn, b % 2, kc, g // 2, 2 * (g % 2):2 * (g % 2) + 2, :]
                    i = nc.tensor.matmul(PS[:, bk, 0:hg * S], v, PT[0:kn, kc, g * hg * S:(g + 1) * hg * S],
                                         start=kc == 0, stop=kc == last)
                i.then_inc(products_ready, mark("pe", f"{t} o{b} {g}"))

        def pe_attention(pe, t, src, ready):
            for c in range(DC):
                if due(f"{ready}{c}"):
                    pe.wait_ge(producer(f"{ready}{c}"), at(f"{ready}{c}"))
            pe_linear(pe, f"{t} q ", sq(WN[t][0]), chunks(src), N)
            if ATT[t]["self"]:
                pe_linear(pe, f"{t} k ", sq(WN[t][1]), chunks(src), N)
                if due(f"{t} k 1 out"):
                    pe.wait_ge(act_results, at(f"{t} k 1 out"))
            pe_kv(pe, t, 0)
            pe_max(pe, t, 0)
            for b in range(GB):
                if b + 1 < GB:
                    pe_kv(pe, t, b + 1)
                    pe_max(pe, t, b + 1)
                pe_scores(pe, t, b)
                pe_values(pe, t, b)

        def pe_norm(pe, t, mean=True):
            if mean:
                for c in range(DC):
                    if due(f"{t} y{c}"):
                        pe.wait_ge(dve_results, at(f"{t} y{c}"))
                pe_linear(pe, f"{t} mu ", lambda k, m: ONEM[:, :], chunks(T1), N, ms=1)
            for c in range(DC):
                if due(f"{t} sq{c}"):
                    pe.wait_ge(act_results, at(f"{t} sq{c}"))
            pe_linear(pe, f"{t} var ", lambda k, m: ONEM[:, :], chunks(T2), N, ms=1)

        def pe_down(pe, use, lhs, made="h{}"):
            for m in range(DC):
                bk = rings["lin"].take(pe, f"{use}{m}", f"{use}{m} out")
                for k in range(8):
                    if due(use + made.format(k)):
                        pe.wait_ge(producer(use + made.format(k)), at(use + made.format(k)))
                    i = nc.tensor.matmul(PS[:, bk, 0:N], lhs(k, m), H[:, k, :], start=k == 0, stop=k == 7)
                i.then_inc(products_ready, mark("pe", f"{use}{m}"))

        def pe_swiglu(pe, t, wg, wu, wd, ready):
            for c in range(DC):
                if due(f"{ready}{c}"):
                    pe.wait_ge(dve_results, at(f"{ready}{c}"))
            for m in range(8):
                for n, ww in (("g", wg), ("u", wu)):
                    bk = rings["lin" if n == "g" else "max"].take(pe, f"{t} {n}{m}", f"{t} {n}{m} out")
                    for k in range(DC):
                        i = nc.tensor.matmul(PS[:, bk, 0:N], w(ww, k, m * P, (m + 1) * P, FF), X[:, k, :], start=k == 0, stop=k == DC - 1)
                    i.then_inc(products_ready, mark("pe", f"{t} {n}{m}"))
            pe_down(pe, f"{t} ", lambda k, m: w(wd, k, m * P, (m + 1) * P))

        def pe_ctx(pe, b, ring="lin"):
            if due(f"ctx{b}"):
                pe.wait_ge(ctx_loaded, at(f"ctx{b}"))
            for c in range(DC):
                bk = rings[ring].take(pe, f"ct{b} {c}", f"ct{b} {c} out")
                for kc, (k0, kn) in enumerate(KCH):
                    i = nc.tensor.transpose(PS[:, bk, k0:k0 + kn], CST[0:kn, kc, c * P:(c + 1) * P], IDENT[0:kn, 0:kn])
                i.then_inc(products_ready, mark("pe", f"ct{b} {c}"))

        def program_pe(pe):
            enter(pe, "prepare", 0)
            rings_start()
            if due("src"):
                pe.wait_ge(fold_sources_loaded, at("src"))
            if due("vectors"):
                pe.wait_ge(constants_loaded, at("vectors"))
            src = lambda o, k: PQ[:, o + k * D:o + (k + 1) * D]
            for f, (name, b1, b2) in enumerate(FOLDS):
                o = f * FOLD_SRC
                for m in range(DC):
                    bk = rings["lin"].take(pe, f"fold {name}{m}", f"fold {name}{m} out")
                    for k in range(DC):
                        i = nc.tensor.matmul(PS[:, bk, 0:D], src(o, k)[:, m * P:(m + 1) * P], src(o + SQ, k), start=k == 0, stop=k == DC - 1)
                    i.then_inc(products_ready, mark("pe", f"fold {name}{m}"))
                    bk = rings["max"].take(pe, f"bias {name}{m}", f"bias {name}{m} out")
                    for k in range(DC):
                        i = nc.tensor.matmul(PS[:, bk, 0:1], src(o + SQ, k)[:, m * P:(m + 1) * P], vec(b1, k), start=k == 0, stop=k == DC - 1)
                    i.then_inc(products_ready, mark("pe", f"bias {name}{m}"))
            o = len(FOLDS) * FOLD_SRC
            for m in range(DC):
                bk = rings["lin"].take(pe, f"fold k2{m}", f"fold k2{m} out")
                for k in range(DC):
                    i = nc.tensor.matmul(PS[:, bk, 0:64], src(o, k)[:, m * P:(m + 1) * P], PQ[:, o + SQ + k * 64:o + SQ + (k + 1) * 64],
                                         start=k == 0, stop=k == DC - 1)
                i.then_inc(products_ready, mark("pe", f"fold k2{m}"))
            bk = rings["max"].take(pe, "bias k2", "bias k2 out")
            for k in range(DC):
                i = nc.tensor.matmul(PS[0:64, bk, 0:1], PQ[:, o + SQ + k * 64:o + SQ + (k + 1) * 64], vec("bk", k), start=k == 0, stop=k == DC - 1)
            i.then_inc(products_ready, mark("pe", "bias k2"))
            if due("w0"):
                pe.wait_ge(weights_loaded, at("w0"))
            if due("w2"):
                pe.wait_ge(weights_loaded, at("w2"))
            for name, ww, bv in (("so", "so", "d_sv"), ("co", "co", "d_cv"), ("o2", "awo", "abv")):
                if name != "o2":
                    if due(f"bias {bv[2:]}1 out"):
                        pe.wait_ge(dve_results, at(f"bias {bv[2:]}1 out"))
                for m in range(DC):
                    bk = rings["max"].take(pe, f"bias {name}{m}", f"bias {name}{m} out")
                    for k in range(DC):
                        i = nc.tensor.matmul(PS[:, bk, 0:1], w(ww, k, m * P, (m + 1) * P), vec(bv, k), start=k == 0, stop=k == DC - 1)
                    i.then_inc(products_ready, mark("pe", f"bias {name}{m}"))

            with pe.Fori(0, NG) as it:
                enter(pe, "group", it)
                rings_start()
                if due("x"):
                    pe.wait_ge(x_loaded, at("x"))
                for c in range(DC):
                    bk = rings["lin"].take(pe, f"xt {c}", f"xt {c} out")
                    for b in range(GB):
                        i = nc.tensor.transpose(PS[:, bk, b * S:(b + 1) * S], XST[0:S, b, c * P:(c + 1) * P], IDENT[0:S, 0:S])
                    i.then_inc(products_ready, mark("pe", f"xt {c}"))
                for b in range(GB):
                    pe_ctx(pe, b)
                pe_attention(pe, "s0", X, "xr0 ")
                if due("s0 o done"):
                    pe.wait_ge(dve_results, at("s0 o done"))
                pe_linear(pe, "s0 w ", sq("so"), chunks(QO), N)
                pe_norm(pe, "n1")
                pe_attention(pe, "c0", X, "n1 x")
                if due("c0 o done"):
                    pe.wait_ge(dve_results, at("c0 o done"))
                pe_linear(pe, "c0 w ", sq("co"), chunks(QO), N)
                pe_norm(pe, "n2")
                for c in range(DC):
                    if due(f"n2 x{c}"):
                        pe.wait_ge(act_results, at(f"n2 x{c}"))
                for m in range(8):
                    bk = rings["lin"].take(pe, f"f0 h{m}", f"f0 h{m} out")
                    for k in range(DC):
                        i = nc.tensor.matmul(PS[:, bk, 0:N], w("ff1", k, m * P, (m + 1) * P, FF), X[:, k, :], start=k == 0, stop=k == DC - 1)
                    i.then_inc(products_ready, mark("pe", f"f0 h{m}"))
                pe_down(pe, "f0 ", lambda k, m: w("ff2", k, m * P, (m + 1) * P), "h{} out")
                pe_norm(pe, "n3")
                pe_attention(pe, "s1", X, "n3 x")
                if due("s1 o done"):
                    pe.wait_ge(dve_results, at("s1 o done"))
                pe_linear(pe, "s1 w ", sq("l1_so"), chunks(QO), N)
                pe_swiglu(pe, "f1", "g1", "u1", "d1", "s1 x")
                pe_attention(pe, "c1", X, "f1 x")
                if due("c1 o done"):
                    pe.wait_ge(dve_results, at("c1 o done"))
                pe_linear(pe, "c1 w ", sq("l1_co"), chunks(QO), N)
                pe_swiglu(pe, "f2", "g2", "u2", "d2", "c1 x")
                pe_norm(pe, "r1", mean=False)
                for c in range(DC):
                    if due(f"r1 x{c}"):
                        pe.wait_ge(dve_results, at(f"r1 x{c}"))
                pe_linear(pe, "z ", sq("z"), chunks(T1), N)
                for use, ww, src2 in (("ga ", "wg1", T2), ("gb ", "k2", T1)):
                    if use == "ga ":
                        if due("z 0 out"):
                            pe.wait_ge(act_results, at("z 0 out"))
                        if due("z 1 out"):
                            pe.wait_ge(act_results, at("z 1 out"))
                    bk = rings["lin"].take(pe, use, use + "out")
                    for k in range(DC):
                        o = WAT[ww] + k * 64
                        i = nc.tensor.matmul(PS[0:64, bk, 0:N], WT[:, o:o + 64], src2[:, k, :], start=k == 0, stop=k == DC - 1)
                    i.then_inc(products_ready, mark("pe", use))
                pe_linear(pe, "gz ", sq("gz"), chunks(T2), N)
                if due("ga out"):
                    pe.wait_ge(act_results, at("ga out"))
                pe_linear(pe, "gA ", lambda k, m: w("wg2", 0, m * P, (m + 1) * P, rows=64), [GH[0:64, 0, :]], N)
                if due("gb out"):
                    pe.wait_ge(act_results, at("gb out"))
                pe_linear(pe, "gB ", lambda k, m: w("gc2", 0, m * P, (m + 1) * P, rows=64), [GH[0:64, 1, :]], N)
                pe_attention(pe, "c2", T1, "r1 x")
                if due("c2 o done"):
                    pe.wait_ge(dve_results, at("c2 o done"))
                pe_linear(pe, "c2 w ", lambda k, m: w("awo" if k < DC else "v2", k % DC, m * P, (m + 1) * P), chunks(QO) + chunks(T1), N)

            enter(pe, "load", 0)
            with pe.Fori(0, S // 2) as it:
                enter(pe, "scan", it)
                for s in range(2):
                    for m in range(DC):
                        if s == 1 and m == 0:
                            if due("pre0"):
                                pe.wait_ge(dve_results, at("pre0"))
                    for m in range(DC):
                        bk = 2 * s + m
                        if s:
                            if due("h0"):
                                pe.wait_ge(dve_results, at("h0"))
                        for k in range(DC):
                            i = nc.tensor.matmul(PS[:, bk, 0:B], tw("wgh", k, m * P, (m + 1) * P), HC[:, s, k, :], start=k == 0, stop=k == DC - 1)
                    i.then_inc(products_ready, mark("pe", f"gates{s}"))

            with pe.Fori(0, NG) as it:
                enter(pe, "tail", it)
                rings_start()
                pe_norm(pe, "r2", mean=False)
                for c in range(DC):
                    if due(f"r2 x{c}"):
                        pe.wait_ge(dve_results, at(f"r2 x{c}"))
                for m in range(8):
                    bk = rings["lin"].take(pe, f"ft h{m}", f"ft h{m} out")
                    for k in range(DC):
                        i = nc.tensor.matmul(PS[:, bk, 0:N], tw("f1", k, m * P, (m + 1) * P, FF), T1[:, k, :], start=k == 0, stop=k == DC - 1)
                    i.then_inc(products_ready, mark("pe", f"ft h{m}"))
                for m in range(DC):
                    bk = rings["lin"].take(pe, f"ft {m}", f"ft x{m}")
                    for k in range(8):
                        if due(f"ft h{k} out"):
                            pe.wait_ge(act_results, at(f"ft h{k} out"))
                        i = nc.tensor.matmul(PS[:, bk, 0:N], tw("f2", k, m * P, (m + 1) * P), H[:, k, :], start=k == 0, stop=k == 7)
                    i.then_inc(products_ready, mark("pe", f"ft {m}"))
                for b in range(GB):
                    pe_ctx(pe, b)
                    for c in range(DC):
                        if due(f"ct{b} {c} out"):
                            pe.wait_ge(act_results, at(f"ct{b} {c} out"))
                        if due(f"ft x{c}"):
                            pe.wait_ge(dve_results, at(f"ft x{c}"))
                    bk = rings["max"].take(pe, f"l3 s{b}", f"l3 p{b}")
                    for c in range(DC):
                        i = nc.tensor.matmul(PS[0:S, bk, 0:C], X[:, c, b * S:(b + 1) * S], CT[:, b, c, :], start=c == 0, stop=c == DC - 1)
                    i.then_inc(products_ready, mark("pe", f"l3 s{b}"))
                    if due(f"l3 pn{b}"):
                        pe.wait_ge(dve_results, at(f"l3 pn{b}"))
                    bk = rings["st"].take(pe, f"l3 pt{b}", f"l3 pt{b} out")
                    for kc, (k0, kn) in enumerate(KCH):
                        i = nc.tensor.transpose(PS[0:kn, bk, kc * S:(kc + 1) * S], PL3[0:S, k0:k0 + kn], IDENT[0:S, 0:S])
                    i.then_inc(products_ready, mark("pe", f"l3 pt{b}"))
                    if due(f"l3 pt{b} out"):
                        pe.wait_ge(act_results, at(f"l3 pt{b} out"))
                    bk = rings["pv"].take(pe, f"l3 ti{b}", f"l3 ti{b} out")
                    for c in range(DC):
                        for kc, (k0, kn) in enumerate(KCH):
                            i = nc.tensor.matmul(PS[:, bk, c * S:(c + 1) * S], CST[0:kn, kc, c * P:(c + 1) * P], PT[0:kn, kc, 0:S],
                                                 start=kc == 0, stop=kc == 2)
                    i.then_inc(products_ready, mark("pe", f"l3 ti{b}"))
                if due(f"l3 ti{GB - 1} out"):
                    pe.wait_ge(act_results, at(f"l3 ti{GB - 1} out"))
                pe_linear(pe, "l3 y ", lambda k, m: tw("trans", k, m * P, (m + 1) * P), chunks(X) + chunks(T1), N)
                for m in range(DC):
                    if due(f"l3 r{m}"):
                        pe.wait_ge(dve_results, at(f"l3 r{m}"))
                for b in range(GB):
                    bk = rings["max"].take(pe, f"l3 out{b}", f"l3 out{b} out")
                    for m in range(DC):
                        i = nc.tensor.transpose(PS[0:S, bk, m * P:(m + 1) * P], T2[:, m, b * S:(b + 1) * S], IDENT)
                    i.then_inc(products_ready, mark("pe", f"l3 out{b}"))

        def act_evac(act, use, out, func=ACT.Identity, rows=P, n=N, point=None, **kw):
            if due(use):
                act.wait_ge(products_ready, at(use))
            nc.scalar.activation(out, PS[0:rows, bank(use), 0:n], func, **kw).then_inc(act_results, mark("act", point or f"{use} out"))

        def act_attention(act, t):
            a = ATT[t]
            for m in range(DC):
                kw = {"bias": vec(QBIAS[t], m)} if t in QBIAS else {}
                act_evac(act, f"{t} q {m}", QO[:, m, :], scale=QSC[t], **kw)
            if a["self"]:
                for m in range(DC):
                    kw = {"bias": vec(KBIAS[t], m)} if t in KBIAS else {}
                    act_evac(act, f"{t} k {m}", K2[:, m, :], **kw)

            def kv(b):
                if b >= 2:
                    if due(f"{t} st{b - 2} {len(a['keys']) - 1} {a['heads'] // 4 - 1}"):
                        act.wait_ge(products_ready, at(f"{t} st{b - 2} {len(a['keys']) - 1} {a['heads'] // 4 - 1}"))
                if not a["self"]:
                    for m in range(DC):
                        kw = {"bias": vec(KBIAS[t], m)} if t in KBIAS else {}
                        act_evac(act, f"{t} k{b} {m}", KC[:, b % 2, m, :], n=C, **kw)
                if b >= 2:
                    if due(f"{t} o{b - 2} 3"):
                        act.wait_ge(products_ready, at(f"{t} o{b - 2} 3"))
                for kc, (k0, kn) in enumerate(a["keys"]):
                    if due(f"{t} v{b} {kc}"):
                        act.wait_ge(products_ready, at(f"{t} v{b} {kc}"))
                    src = PS[0:kn, bank(f"{t} v{b} {kc}"), 0:D].rearrange("p (c s i) -> p c s i", c=DC, s=2)
                    nc.scalar.activation(VA[0:kn, b % 2, kc, :, 0:4:3, :], src, ACT.Copy).then_inc(act_results, mark("act", f"{t} v{b} {kc} out"))

            kv(0)
            for b in range(GB):
                if b + 1 < GB:
                    kv(b + 1)
                for kc, (k0, kn) in enumerate(a["keys"]):
                    for u in range(a["heads"] // 4):
                        if b and kc == 0 and u == 0:
                            if due(f"{t} o{b - 1} 3"):
                                act.wait_ge(products_ready, at(f"{t} o{b - 1} 3"))
                        if due(f"{t} st{b} {kc} {u}"):
                            act.wait_ge(products_ready, at(f"{t} st{b} {kc} {u}"))
                        nc.scalar.activation(PT[0:kn, kc, u * N:(u + 1) * N], PS[0:kn, bank(f"{t} st{b} {kc} {u}"), 0:N], ACT.Exp).then_inc(act_results, mark("act", f"{t} p{b} {kc} {u}"))

        def act_norm(act, t, eps, gain=None, bias=None, mean=True, src=None):
            for c in range(DC):
                if due(f"{t} c{c}"):
                    act.wait_ge(dve_results, at(f"{t} c{c}"))
                nc.scalar.activation(T2[:, c, :], (T1 if mean else X)[:, c, :], ACT.Square).then_inc(act_results, mark("act", f"{t} sq{c}"))
            if due(f"{t} var 0"):
                act.wait_ge(products_ready, at(f"{t} var 0"))
            nc.scalar.activation(T2[:, 0, :], PS[:, bank(f"{t} var 0"), 0:N], ACT.Sqrt, bias=EPS[:, eps:eps + 1]).then_inc(act_results, mark("act", f"{t} var 0 out"))
            if gain:
                for c in range(DC):
                    if due(f"{t} t{c}"):
                        act.wait_ge(dve_results, at(f"{t} t{c}"))
                    nc.scalar.activation(X[:, c, :], T1[:, c, :], ACT.Identity, scale=vec(gain, c), bias=vec(bias, c)).then_inc(act_results, mark("act", f"{t} x{c}"))

        def act_swiglu(act, t):
            for m in range(8):
                if m >= 2:
                    if due(f"{t} h{m - 2}"):
                        act.wait_ge(dve_results, at(f"{t} h{m - 2}"))
                act_evac(act, f"{t} g{m}", U[:, m % 2, :], func=ACT.Silu)

        def act_ctx(act, b):
            for c in range(DC):
                act_evac(act, f"ct{b} {c}", CT[:, b, c, :], n=C, func=ACT.Copy)

        def program_act(act):
            enter(act, "prepare", 0)
            for name, _, _ in FOLDS:
                for m in range(DC):
                    o = WAT[name] + m * D
                    act_evac(act, f"fold {name}{m}", WT[:, o:o + D], n=D, func=ACT.Copy)
            for m in range(DC):
                o = WAT["k2"] + m * 64
                act_evac(act, f"fold k2{m}", WT[:, o:o + 64], n=64, func=ACT.Copy)

            with act.Fori(0, NG) as it:
                enter(act, "group", it)
                for c in range(DC):
                    act_evac(act, f"xt {c}", X[:, c, :], func=ACT.Copy)
                    book.marks["group", f"xr0 {c}"] = book.marks["group", f"xt {c} out"]
                for b in range(GB):
                    act_ctx(act, b)
                act_attention(act, "s0")
                act_norm(act, "n1", 0, "ln1_g", "ln1_b")
                act_attention(act, "c0")
                act_norm(act, "n2", 0, "ln2_g", "ln2_b")
                for m in range(8):
                    act_evac(act, f"f0 h{m}", H[:, m, :], func=ACT.Gelu, bias=vec("ff_b1", m))
                act_norm(act, "n3", 0, "ln3_g", "ln3_b")
                act_attention(act, "s1")
                act_swiglu(act, "f1")
                act_attention(act, "c1")
                act_swiglu(act, "f2")
                act_norm(act, "r1", 1, mean=False)
                if due("r1 x1"):
                    act.wait_ge(dve_results, at("r1 x1"))
                for m in range(DC):
                    act_evac(act, f"z {m}", T2[:, m, :], bias=vec("bz", m))
                act_evac(act, "ga ", GH[0:64, 0, :], rows=64, func=ACT.Gelu_apprx_tanh, bias=vec("bg1", rows=64), point="ga out")
                act_evac(act, "gb ", GH[0:64, 1, :], rows=64, func=ACT.Gelu_apprx_tanh, bias=vec("d_k2", rows=64), point="gb out")
                for m in range(DC):
                    act_evac(act, f"gz {m}", GZ[:, m, :], bias=vec("d_gz", m))
                for m in range(DC):
                    act_evac(act, f"gA {m}", SG[:, m, :], func=ACT.Sigmoid, bias=vec("bg2", m))
                for m in range(DC):
                    act_evac(act, f"gB {m}", GM[:, m, :], func=ACT.Sigmoid, bias=vec("bgc2", m))
                if due("spill gm"):
                    act.wait_ge(spilled, at("spill gm"))
                act_attention(act, "c2")

            enter(act, "load", 0)
            with act.Fori(0, S // 2) as it:
                enter(act, "scan", it)
                for s in range(2):
                    if due(f"pre{s}"):
                        act.wait_ge(dve_results, at(f"pre{s}"))
                    nc.scalar.activation(GA[:, :, :], GA[:, :, :], ACT.Sigmoid).then_inc(act_results, mark("act", f"gate{s}"))

            with act.Fori(0, NG) as it:
                enter(act, "tail", it)
                act_norm(act, "r2", 1, mean=False)
                for m in range(8):
                    act_evac(act, f"ft h{m}", H[:, m, :], func=ACT.Gelu_apprx_tanh, bias=vec("bf1", m))
                for b in range(GB):
                    act_ctx(act, b)
                    if due(f"l3 m{b}"):
                        act.wait_ge(dve_results, at(f"l3 m{b}"))
                    if b:
                        if due(f"l3 pt{b - 1}"):
                            act.wait_ge(products_ready, at(f"l3 pt{b - 1}"))
                    nc.scalar.activation(PL3[0:S, :], PS[0:S, bank(f"l3 s{b}"), 0:C], ACT.Exp, bias=MX[:, 0, 0:1],
                                             accum_out=MX[:, 0, 1:2]).then_inc(act_results, mark("act", f"l3 p{b}"))
                    for kc, (k0, kn) in enumerate(KCH):
                        if due(f"l3 pt{b}"):
                            act.wait_ge(products_ready, at(f"l3 pt{b}"))
                        if b:
                            if due(f"l3 ti{b - 1}"):
                                act.wait_ge(products_ready, at(f"l3 ti{b - 1}"))
                        i = nc.scalar.activation(PT[0:kn, kc, 0:S], PS[0:kn, bank(f"l3 pt{b}"), kc * S:(kc + 1) * S], ACT.Copy)
                    i.then_inc(act_results, mark("act", f"l3 pt{b} out"))
                    if due(f"l3 ti{b}"):
                        act.wait_ge(products_ready, at(f"l3 ti{b}"))
                    src = PS[:, bank(f"l3 ti{b}"), 0:DC * S].rearrange("p (c n) -> p c n", c=DC)
                    nc.scalar.activation(T1[:, :, b * S:(b + 1) * S], src, ACT.Copy).then_inc(act_results, mark("act", f"l3 ti{b} out"))
                for m in range(DC):
                    act_evac(act, f"l3 y {m}", T2[:, m, :], func=ACT.Tanh, bias=vec("trans_b", m))
                for b in range(GB):
                    act_evac(act, f"l3 out{b}", YO[0:S, b, :], rows=S, n=D, func=ACT.Copy)

        def dve_attention(dve, t):
            a = ATT[t]
            hg, heads = a["hg"], a["heads"]

            def maxima(b):
                if b >= 2:
                    if due(f"{t} md{b - 2}"):
                        dve.wait_ge(dve_results, at(f"{t} md{b - 2}"))
                if a["self"]:
                    for u in range(heads // 4):
                        if due(f"{t} s{b} {u}"):
                            dve.wait_ge(products_ready, at(f"{t} s{b} {u}"))
                        src = PS[0:S, bank(f"{t} s{b} {u}"), 0:N].rearrange("p (h k) -> p h k", h=4)
                        nc.vector.reduce_max(MX[:, b % 2, 4 * u:4 * u + 4], src, AX).then_inc(dve_results, mark("dve", f"{t} m{b} {u}"))
                else:
                    for h in range(heads):
                        if due(f"{t} s{b} {h}"):
                            dve.wait_ge(products_ready, at(f"{t} s{b} {h}"))
                        nc.vector.reduce_max(MX[:, b % 2, h:h + 1], PS[0:S, bank(f"{t} s{b} {h}"), 0:C], AX).then_inc(dve_results, mark("dve", f"{t} m{b} {h}"))

            def diagonals(b):
                if b:
                    if due(f"{t} st{b - 1} {len(a['keys']) - 1} {heads // 4 - 1}"):
                        dve.wait_ge(products_ready, at(f"{t} st{b - 1} {len(a['keys']) - 1} {heads // 4 - 1}"))
                if due(f"{t} m{b} {heads // 4 - 1 if a['self'] else heads - 1}"):
                    dve.wait_ge(dve_results, at(f"{t} m{b} {heads // 4 - 1 if a['self'] else heads - 1}"))
                nc.vector.tensor_tensor(MD[:, 0:heads, :], const("negid", S, S).unsqueeze(1).broadcast_to([S, heads, S]),
                                            MX[:, b % 2, 0:heads].unsqueeze(2).broadcast_to([S, heads, S]), ALU.mult).then_inc(dve_results, mark("dve", f"{t} md{b}"))

            def outputs(b):
                for g in range(4):
                    if due(f"{t} o{b} {g}"):
                        dve.wait_ge(products_ready, at(f"{t} o{b} {g}"))
                    src = PS[:, bank(f"{t} o{b} {g}"), 0:hg * S].rearrange("p (h q) -> p h q", h=hg)
                    if b or g:
                        if due(f"{t} {'o' if False else 'x'}{b if g else b - 1} {g - 1 if g else 3}"):
                            dve.wait_ge(dve_results, at(f"{t} {'o' if False else 'x'}{b if g else b - 1} {g - 1 if g else 3}"))
                    if hg == 1:
                        nc.vector.tensor_copy(EX[:, g, :], src[:, 0, :]).then_inc(dve_results, mark("dve", f"{t} e{b} {g}"))
                        mark_same(f"{t} x{b} {g}", f"{t} e{b} {g}")
                        continue
                    em = EM[:, 0:hg * S].rearrange("p (h q) -> p h q", h=hg)
                    msk = const(a["em"], hg).unsqueeze(2).broadcast_to([P, hg, S])
                    nc.vector.tensor_tensor(em, src, msk, ALU.mult).then_inc(dve_results, mark("dve", f"{t} e{b} {g}"))
                    if due(f"{t} e{b} {g}"):
                        dve.wait_ge(dve_results, at(f"{t} e{b} {g}"))
                    nc.vector.reduce_sum(EX[:, g, :], em.rearrange("p h q -> p q h"), AX).then_inc(dve_results, mark("dve", f"{t} x{b} {g}"))
                if due(f"{t} x{b} 3"):
                    dve.wait_ge(dve_results, at(f"{t} x{b} 3"))
                nc.vector.tensor_copy(DN[0:64, :, :], EX[64:128, 0:4:2, :]).then_inc(dve_results, mark("dve", f"{t} dn{b} 0"))
                nc.vector.tensor_copy(DN[64:128, :, :], EX[0:64, 1:4:2, :]).then_inc(dve_results, mark("dve", f"{t} dn{b} 1"))
                if due(f"{t} dn{b} 1"):
                    dve.wait_ge(dve_results, at(f"{t} dn{b} 1"))
                nc.vector.reciprocal(DN[:, :, :], DN[:, :, :]).then_inc(dve_results, mark("dve", f"{t} rc{b}"))
                if due(f"{t} rc{b}"):
                    dve.wait_ge(dve_results, at(f"{t} rc{b}"))
                o = QO[:, :, b * S:(b + 1) * S]
                nc.vector.tensor_tensor(o[0:64], EX[0:64, 0:4:2, :], DN[0:64, :, :], ALU.mult).then_inc(dve_results, mark("dve", f"{t} oo{b} 0"))
                nc.vector.tensor_tensor(o[64:128], EX[64:128, 1:4:2, :], DN[64:128, :, :], ALU.mult).then_inc(dve_results, mark("dve", f"{t} o done" if b == GB - 1 else f"{t} oo{b} 1"))
                if due(f"{t} o done" if b == GB - 1 else f"{t} oo{b} 1"):
                    dve.wait_ge(dve_results, at(f"{t} o done" if b == GB - 1 else f"{t} oo{b} 1"))

            maxima(0)
            diagonals(0)
            for b in range(GB):
                if b + 1 < GB:
                    maxima(b + 1)
                if due(f"{t} qb{min(b + 1, GB - 1)} 1"):
                    dve.wait_ge(pool_results, at(f"{t} qb{min(b + 1, GB - 1)} 1"))
                outputs(b)
                if b + 1 < GB:
                    diagonals(b + 1)

        def mark_same(new, old):
            book.marks[phase["name"], new] = book.marks[phase["name"], old]

        def dve_residual(dve, use, out, bias, point, resid):
            for m in range(DC):
                if due(f"{use}{m}"):
                    dve.wait_ge(products_ready, at(f"{use}{m}"))
                pin = PS[:, bank(f"{use}{m}"), 0:N]
                if bias:
                    i = nc.vector.scalar_tensor_tensor(out[:, m, :], pin, vec(bias, m), resid[:, m, :], ALU.add, ALU.add)
                else:
                    i = nc.vector.tensor_tensor(out[:, m, :], pin, resid[:, m, :], ALU.add)
                i.then_inc(dve_results, mark("dve", f"{point}{m}"))
                mark_same(f"{use}{m} out", f"{point}{m}")

        def dve_center(dve, t):
            if due(f"{t} mu 0"):
                dve.wait_ge(products_ready, at(f"{t} mu 0"))
            for c in range(DC):
                if due(f"{t} y{c}"):
                    dve.wait_ge(dve_results, at(f"{t} y{c}"))
                nc.vector.tensor_tensor(T1[:, c, :], T1[:, c, :], PS[:, bank(f"{t} mu 0"), 0:N], ALU.subtract).then_inc(dve_results, mark("dve", f"{t} c{c}"))
            mark_same(f"{t} mu 0 out", f"{t} c1")
            dve_scale(dve, t)

        def dve_scale(dve, t, gain=None):
            if due(f"{t} var 0 out"):
                dve.wait_ge(act_results, at(f"{t} var 0 out"))
            nc.vector.reciprocal(T2[:, 0, :], T2[:, 0, :]).then_inc(dve_results, mark("dve", f"{t} rs"))
            if due(f"{t} rs"):
                dve.wait_ge(dve_results, at(f"{t} rs"))
            for c in range(DC):
                if gain:
                    nc.vector.scalar_tensor_tensor(T1[:, c, :], X[:, c, :], vec(gain, c), T2[:, 0, :], ALU.mult, ALU.mult).then_inc(dve_results, mark("dve", f"{t} x{c}"))
                else:
                    nc.vector.tensor_tensor(T1[:, c, :], T1[:, c, :], T2[:, 0, :], ALU.mult).then_inc(dve_results, mark("dve", f"{t} t{c}"))

        def dve_swiglu(dve, t):
            for m in range(8):
                if due(f"{t} g{m} out"):
                    dve.wait_ge(act_results, at(f"{t} g{m} out"))
                if due(f"{t} u{m}"):
                    dve.wait_ge(products_ready, at(f"{t} u{m}"))
                nc.vector.tensor_tensor(H[:, m, :], PS[:, bank(f"{t} u{m}"), 0:N], U[:, m % 2, :], ALU.mult).then_inc(dve_results, mark("dve", f"{t} h{m}"))
                mark_same(f"{t} u{m} out", f"{t} h{m}")

        def program_dve(dve):
            enter(dve, "prepare", 0)
            if due("constants"):
                dve.wait_ge(constants_loaded, at("constants"))
            nc.vector.memset(ONEM[:, :], 1.0 / D).then_inc(dve_results, mark("dve", "p0"))
            nc.vector.memset(VA[:, :, :, :, 1:3, :], 1.0).then_inc(dve_results, mark("dve", "p1"))
            nc.vector.memset(EPS[:, 0:1], 1e-5).then_inc(dve_results, mark("dve", "p2"))
            nc.vector.memset(EPS[:, 1:2], 1e-6).then_inc(dve_results, mark("dve", "p3"))
            nc.vector.memset(EM[:, 0:P], 1.0).then_inc(dve_results, mark("dve", "p4"))
            if due("p4"):
                dve.wait_ge(dve_results, at("p4"))
            nc.vector.tensor_copy(ONER[:, :], EM[0:S, 0:P]).then_inc(dve_results, mark("dve", "p6"))
            nc.vector.tensor_copy(IDB[:, :], const("ident", S, S)).then_inc(dve_results, mark("dve", "p7"))
            nc.vector.tensor_copy(NEGB[:, :, :], const("neg", S, S).unsqueeze(1).broadcast_to([S, 4, S])).then_inc(dve_results, mark("dve", "p8"))
            nc.vector.tensor_copy(NEGTB[:, :, :], const("negT", S, S).unsqueeze(1).broadcast_to([S, 4, S])).then_inc(dve_results, mark("dve", "p9"))
            if due("vectors"):
                dve.wait_ge(constants_loaded, at("vectors"))
            for name, _, b2 in FOLDS:
                scale = {"sq": 1 / 16, "cq": 1 / 16, "q2": 1 / math.sqrt(32)}.get(name, 1.0)
                for m in range(DC):
                    if due(f"bias {name}{m}"):
                        dve.wait_ge(products_ready, at(f"bias {name}{m}"))
                    nc.vector.tensor_scalar(vec(f"d_{name}", m), PS[:, bank(f"bias {name}{m}"), 0:1], vec(b2, m), scale, ALU.add, ALU.mult).then_inc(dve_results, mark("dve", f"bias {name}{m} out"))
            if due("bias k2"):
                dve.wait_ge(products_ready, at("bias k2"))
            nc.vector.tensor_scalar(vec("d_k2", rows=64), PS[0:64, bank("bias k2"), 0:1], vec("bgc1", rows=64), None, ALU.add).then_inc(dve_results, mark("dve", "bias k2 out"))
            nc.vector.tensor_tensor(VEC[:, VAT["d_gz"]:VAT["d_gz"] + 2], VEC[:, VAT["bgz"]:VAT["bgz"] + 2],
                                        VEC[:, VAT["bgh"]:VAT["bgh"] + 2], ALU.add).then_inc(dve_results, mark("dve", "d_gz"))
            for name, b2 in (("so", "m_bo"), ("co", "c_bo"), ("o2", "abo")):
                for m in range(DC):
                    if due(f"bias {name}{m}"):
                        dve.wait_ge(products_ready, at(f"bias {name}{m}"))
                    nc.vector.tensor_scalar(vec(f"d_{name}", m), PS[:, bank(f"bias {name}{m}"), 0:1], vec(b2, m), None, ALU.add).then_inc(dve_results, mark("dve", f"bias {name}{m} out"))
            if due("bias o21 out"):
                dve.wait_ge(dve_results, at("bias o21 out"))
            for m in range(DC):
                nc.vector.scalar_tensor_tensor(vec("d_o2", m), vec("bv", m), 0.1, vec("d_o2", m), ALU.mult, ALU.add).then_inc(dve_results, mark("dve", f"dd{m}"))
            if due("w2"):
                dve.wait_ge(weights_loaded, at("w2"))
            o = WAT["v2"]
            nc.vector.tensor_scalar(WT[:, o:o + SQ], WT[:, o:o + SQ], 0.1, None, ALU.mult).then_inc(dve_results, mark("dve", "v2"))

            with dve.Fori(0, NG) as it:
                enter(dve, "group", it)
                dve_attention(dve, "s0")
                dve_residual(dve, "s0 w ", T1, "d_so", "n1 y", X)
                dve_center(dve, "n1")
                dve_attention(dve, "c0")
                dve_residual(dve, "c0 w ", T1, "d_co", "n2 y", X)
                dve_center(dve, "n2")
                dve_residual(dve, "f0 ", T1, "ff_b2", "n3 y", X)
                dve_center(dve, "n3")
                dve_attention(dve, "s1")
                dve_residual(dve, "s1 w ", X, None, "s1 x", X)
                dve_swiglu(dve, "f1")
                dve_residual(dve, "f1 ", X, None, "f1 x", X)
                dve_attention(dve, "c1")
                dve_residual(dve, "c1 w ", X, None, "c1 x", X)
                dve_swiglu(dve, "f2")
                dve_residual(dve, "f2 ", X, None, "r1 c", X)
                dve_scale(dve, "r1", gain="norm1")
                for m in range(DC):
                    if due(f"gB {m} out"):
                        dve.wait_ge(act_results, at(f"gB {m} out"))
                    nc.vector.tensor_tensor(GM[:, m, :], GM[:, m, :], SG[:, m, :], ALU.mult).then_inc(dve_results, mark("dve", f"gm a{m}"))
                    if due(f"gm a{m}"):
                        dve.wait_ge(dve_results, at(f"gm a{m}"))
                    nc.vector.tensor_scalar(GM[:, m, :], GM[:, m, :], 1e-6, 1.0 - 1e-6, ALU.max, ALU.min).then_inc(dve_results, mark("dve", f"gm b{m}"))
                    if due(f"gm b{m}"):
                        dve.wait_ge(dve_results, at(f"gm b{m}"))
                    nc.vector.tensor_scalar(GM[:, m, :], GM[:, m, :], 1.0, None, ALU.add).then_inc(dve_results, mark("dve", f"gm{m}"))
                dve_attention(dve, "c2")
                dve_residual(dve, "c2 w ", X, "d_o2", "base", X)

            enter(dve, "load", 0)
            nc.vector.memset(HC[:, 0, :, :], 0.0).then_inc(dve_results, mark("dve", "h at rest"))

            def steps(name, t):
                return seq(name).rearrange("p (c b t) -> p c b t", c=DC, b=B)[:, :, :, bass.ds(t, 1)]

            with dve.Fori(0, S // 2) as it:
                enter(dve, "scan", it)
                for s in range(2):
                    h = HC[:, s, :, :].unsqueeze(3)
                    t = it * 2 + s
                    if s:
                        if due("h0"):
                            dve.wait_ge(dve_results, at("h0"))
                    nc.vector.tensor_tensor(ZH[:, :, :].unsqueeze(3), steps("zs", t), h, ALU.subtract).then_inc(dve_results, mark("dve", f"zh{s}"))
                    nc.vector.tensor_tensor(HG[:, :, :].unsqueeze(3), steps("gms", t), h, ALU.mult).then_inc(dve_results, mark("dve", f"hg{s}"))
                    if due(f"gates{s}"):
                        dve.wait_ge(products_ready, at(f"gates{s}"))
                    nc.vector.tensor_tensor(GA[:, :, :].unsqueeze(3), PS[:, 2 * s:2 * s + 2, 0:B].unsqueeze(3), steps("gzs", t), ALU.add).then_inc(dve_results, mark("dve", f"pre{s}"))
                    if due(f"gate{s}"):
                        dve.wait_ge(act_results, at(f"gate{s}"))
                    nc.vector.tensor_tensor(GU[:, :, :], GA[:, :, :], ZH[:, :, :], ALU.mult).then_inc(dve_results, mark("dve", f"gu{s}"))
                    if due(f"gu{s}"):
                        dve.wait_ge(dve_results, at(f"gu{s}"))
                    nc.vector.tensor_tensor(HC[:, 1 - s, :, :], GU[:, :, :], HG[:, :, :], ALU.add).then_inc(dve_results, mark("dve", f"h{s}"))

            with dve.Fori(0, NG) as it:
                enter(dve, "tail", it)
                for c in range(DC):
                    o = lambda name: seq(name)[:, bass.ds(it * N + c * B * S, N)]
                    nc.vector.tensor_tensor(X[:, c, :], o("base"), o("hs"), ALU.add).then_inc(dve_results, mark("dve", f"r2 c{c}"))
                dve_scale(dve, "r2", gain="norm2")
                dve_residual(dve, "ft ", X, "bf2", "ft x", X)
                for b in range(GB):
                    if due(f"l3 s{b}"):
                        dve.wait_ge(products_ready, at(f"l3 s{b}"))
                    if b:
                        if due(f"l3 pn{b - 1}"):
                            dve.wait_ge(dve_results, at(f"l3 pn{b - 1}"))
                    nc.vector.tensor_reduce(MX[:, 0, 0:1], PS[0:S, bank(f"l3 s{b}"), 0:C], AX, ALU.max, negate=True).then_inc(dve_results, mark("dve", f"l3 m{b}"))
                    if due(f"l3 p{b}"):
                        dve.wait_ge(act_results, at(f"l3 p{b}"))
                    nc.vector.reciprocal(MX[:, 0, 1:2], MX[:, 0, 1:2]).then_inc(dve_results, mark("dve", f"l3 rc{b}"))
                    if due(f"l3 rc{b}"):
                        dve.wait_ge(dve_results, at(f"l3 rc{b}"))
                    nc.vector.tensor_scalar(PL3[0:S, :], PL3[0:S, :], MX[:, 0, 1:2], None, ALU.mult).then_inc(dve_results, mark("dve", f"l3 pn{b}"))
                for m in range(DC):
                    if due(f"l3 y {m} out"):
                        dve.wait_ge(act_results, at(f"l3 y {m} out"))
                    nc.vector.tensor_tensor(T2[:, m, :], T2[:, m, :], X[:, m, :], ALU.add).then_inc(dve_results, mark("dve", f"l3 r{m}"))

        def program_pool(pool):
            enter(pool, "prepare", 0)
            nc.gpsimd.memset(QO[:, 0, 0:1], 0.0).then_inc(pool_results, mark("pool", "begun"))
            with pool.Fori(0, NG) as it:
                enter(pool, "group", it)
                for t in ("s0", "c0", "s1", "c1", "c2"):
                    a = ATT[t]
                    hc = a["hc"]
                    if due(f"{t} q 1 out"):
                        pool.wait_ge(act_results, at(f"{t} q 1 out"))
                    for b in range(GB):
                        if b >= 2:
                            if due(f"{t} st{b - 2} {len(a['keys']) - 1} {a['heads'] // 4 - 1}"):
                                pool.wait_ge(products_ready, at(f"{t} st{b - 2} {len(a['keys']) - 1} {a['heads'] // 4 - 1}"))
                        for c in range(DC):
                            nc.gpsimd.tensor_tensor(QB[:, b % 2, c, 0:hc * S].rearrange("p (h q) -> p h q", h=hc),
                                                        QO[:, c, b * S:(b + 1) * S].unsqueeze(1).broadcast_to([P, hc, S]),
                                                        const(a["mask"], hc).unsqueeze(2).broadcast_to([P, hc, S]), ALU.mult).then_inc(pool_results, mark("pool", f"{t} qb{b} {c}"))
            enter(pool, "load", 0)
            with pool.Fori(0, S // 2) as it:
                enter(pool, "scan", it)
                for s in range(2):
                    if due(f"h{s}"):
                        pool.wait_ge(dve_results, at(f"h{s}"))
                    dst = seq("hs").rearrange("p (c b t) -> p c b t", c=DC, b=B)[:, :, :, bass.ds(it * 2 + s, 1)]
                    nc.gpsimd.tensor_copy(dst, HC[:, 1 - s, :, :].unsqueeze(3)).then_inc(pool_results, mark("pool", f"hs{s}"))

        def load_ctx(sp, row, b, used):
            if b:
                if due(used):
                    sp.wait_ge(products_ready, at(used))
            for kc, (k0, kn) in enumerate(KCH):
                src = ctx_in[bass.ds(row, 1), k0:k0 + kn, :].rearrange("a k d -> (a k) d")
                sp.dma_start(CST[0:kn, kc, :], src).then_inc(ctx_loaded, mark("ctx", f"ctx{b}" if kc == 2 else f"ctx{b} {kc}", 16))

        def program_sp(sp):
            enter(sp, "prepare", 0)
            for track in ("x", "ctx", "spill", "out"):
                sp.sem_inc(sems[track], mark(track, f"{track} begun", 16))
            sp.dma_start(VEC[:, 0:NVEC_IN], vec_in).then_inc(constants_loaded, mark("cst", "vectors0", 16))
            sp.dma_start(CO[:, :], const_in).then_inc(constants_loaded, mark("cst", "constants", 16))
            mark_same("vectors", "constants")
            sp.dma_start(PQ[:, 0:NSRC], src_in).then_inc(fold_sources_loaded, mark("src", "src", 16))
            sp.dma_start(WT[:, NWF:NWF + NW0], w0_in).then_inc(weights_loaded, mark("w", "w0a", 16))
            sp.dma_start(WT[:, NWF + NW0 + NW1:NW], w2_in).then_inc(weights_loaded, mark("w", "w2", 16))
            mark_same("w0", "w2")
            sp.dma_start(WT[:, NWF + NW0:NWF + NW0 + NW1], w1_in).then_inc(weights1_loaded, mark("w1", "w1", 16))
            with sp.Fori(0, NG) as it:
                rows_at = [sp.snap(it * GB + b) for b in range(GB)]
                col_at = sp.snap(it * N)
                enter(sp, "group", it, ("pe", "act", "dve"))
                sp.dma_start(XST[0:S, :, :], x_in[bass.ds(rows_at[0], GB), :, :].rearrange("b s d -> s b d")).then_inc(x_loaded, mark("x", "x", 16))
                for b in range(GB):
                    load_ctx(sp, rows_at[b], b, f"ct{b - 1} 1")
                for k, (name, t, points) in enumerate((("z", T2, ("z 1 out",)), ("gz", GZ, ("gz 1 out",)), ("gm", GM, ("gm1",)), ("base", X, ("base1",)))):
                    for p in points:
                        if due(p):
                            sp.wait_ge(producer(p), at(p))
                    sp.dma_start(spill[k, :, :, bass.ds(col_at, N)], t[:, :, :]).then_inc(spilled, mark("spill", f"spill {name}", 16))
            enter(sp, "load", 0)
            sp.dma_start(WT[:, 0:NTW], tw_in).then_inc(sequences_loaded, mark("seq", "tw", 16))
            for k, name in enumerate(("zs", "gzs", "gms", "base")):
                sp.dma_start(seq(name).rearrange("p (c n) -> p c n", c=DC), spill[k]).then_inc(sequences_loaded, mark("seq", f"ld {name}", 16))
            with sp.Fori(0, NG) as it:
                rows_at = [sp.snap(it * GB + b) for b in range(GB)]
                enter(sp, "tail", it, ("pe",))
                for b in range(GB):
                    load_ctx(sp, rows_at[b], b, f"l3 ti{b - 1}")
                if due(f"l3 out{GB - 1} out"):
                    sp.wait_ge(act_results, at(f"l3 out{GB - 1} out"))
                sp.dma_start(out[bass.ds(rows_at[0], GB), :, :].rearrange("b s d -> s b d"), YO[0:S, :, :]).then_inc(outputs_stored, mark("out", "out", 16))
            if known:
                sp.wait_ge(outputs_stored, NG * 16 + 16)

        block = ctx.enter_context(nc.Block())

        @block.sync
        def _(sp):
            program_sp(sp)

        @block.scalar
        def _(act):
            program_act(act)

        @block.vector
        def _(dve):
            program_dve(dve)

        @block.gpsimd
        def _(pool):
            program_pool(pool)

        @block.tensor
        def _(pe):
            program_pe(pe)


def rows(a):
    k, m = a.shape
    return a.reshape(k // P, P, m).transpose(1, 0, 2).reshape(P, -1)


def column(v):
    if v.size < P:
        v = np.concatenate([v, np.zeros(P - v.size, v.dtype)])
    return v.reshape(-1, P).T


def kernel(**inputs):
    import concourse.bacc as bacc
    from concourse.bass_utils import run_bass_kernel_spmd as run

    i0 = {k[9:]: np.asarray(v) for k, v in inputs.items() if k.startswith("L0_")}
    i1 = {k[9:]: np.asarray(v) for k, v in inputs.items() if k.startswith("L1_")}
    i2 = {k[9:]: np.asarray(v) for k, v in inputs.items() if k.startswith("L2_")}
    i3 = {k[9:]: np.asarray(v) for k, v in inputs.items() if k.startswith("L3_")}
    cat = lambda parts: np.ascontiguousarray(np.concatenate(parts, axis=1))
    vals = dict(i0)
    vals.update({"norm1": i2["norm1_scale"], "norm2": i2["norm2_scale"], "trans_b": i3["trans_b"]})
    for n in ("bq", "bk", "bv", "bz", "bgz", "bgh", "bg2", "bgc2", "abq", "abk", "abv", "abo", "bf2", "bf1", "bg1", "bgc1"):
        vals[n] = i2[n]
    heads = lambda a: a.reshape(D, D).T
    pad64 = lambda a: np.concatenate([a, np.zeros((P - a.shape[0], a.shape[1]), a.dtype)])
    src = []
    for a, b in (("sa_q_W", "m_Wq"), ("sa_k_W", "m_Wk"), ("sa_v_W", "m_Wv"), ("ca_q_W", "c_Wq"), ("ca_k_W", "c_Wk"), ("ca_v_W", "c_Wv")):
        src += [rows(i0[a]), rows(heads(i0[b]))]
    src += [rows(i2["Wq"].T), rows(i2["Awq"]), rows(i2["Wk"].T), rows(i2["Wgc1"])]
    arrays = {
        "x": np.asarray(inputs["x"]), "ctx": np.asarray(inputs["ctx_1024"]),
        "vec": cat([column(vals[n].reshape(-1)) for n, _ in VECS]),
        "const": constants(),
        "src": cat(src),
        "w0": cat([rows(i0["m_Wo"].T), rows(i0["c_Wo"].T), rows(i0["ff_W1"].T), rows(i0["ff_W2"].T)]),
        "w1": cat([rows(i1[n]) for n in ("sa_wq", "sa_wk", "sa_wv", "sa_wo", "samlp_wg", "samlp_wu", "samlp_wd",
                                         "ca_wq", "ca_wk", "ca_wv", "ca_wo", "camlp_wg", "camlp_wu", "camlp_wd")]),
        "w2": cat([rows(i2[n]) for n in ("Wz", "Wgz", "Wv", "Awk", "Awv", "Awo", "Wg1")] + [pad64(i2["Wg2"]), pad64(i2["Wgc2"])]),
        "tw": cat([rows(i2["Wgh"]), rows(i2["Wf1"]), rows(i2["Wf2"]), rows(i3["trans_W"])]),
    }

    def make(book):
        nc = bacc.Bacc("TRN2", target_bir_lowering=False, num_devices=1)
        ins = [nc.dram_tensor(f"in_{n}", a.shape, mybir.dt.from_np(a.dtype), kind="ExternalInput").ap() for n, a in arrays.items()]
        out = nc.dram_tensor("out", (B, S, D), F32, kind="ExternalOutput").ap()
        spill = nc.dram_tensor("spill", (4, P, DC, B * S), F32, kind="Internal").ap()
        build(nc, book, *ins, out, spill)
        return nc

    counted = Book()
    make(counted)
    nc = make(Book(counted))
    r = run(nc, [{f"in_{n}": a for n, a in arrays.items()}], core_ids=[0])
    return r.results[0]["out"]
```

```python
import math
from contextlib import ExitStack

import concourse.bass as bass
import numpy as np
from concourse import mybir

F32 = mybir.dt.float32
F32R = mybir.dt.float32r
BF16 = mybir.dt.bfloat16
ACT = mybir.ActivationFunctionType
ALU = mybir.AluOpType
AX = mybir.AxisListType.X

B, S, C, D, FF = 16, 100, 361, 256, 1024
P = 128
DC = D // P
GB = 4
NG = B // GB
N = GB * S
KCH = [(0, 128), (128, 128), (256, C - 256)]
SCH = [(0, S)]
MASKED = -1.0e30

FOLDS = [("sq", "sa_q_b", "m_bq"), ("sk", "sa_k_b", "m_bk"), ("sv", "sa_v_b", "m_bv"),
         ("cq", "ca_q_b", "c_bq"), ("ck", "ca_k_b", "c_bk"), ("cv", "ca_v_b", "c_bv"), ("q2", "bq", "abq")]

VECS = [(n, DC) for n in ("sa_q_b", "sa_k_b", "sa_v_b", "ca_q_b", "ca_k_b", "ca_v_b",
                          "m_bq", "m_bk", "m_bv", "m_bo", "c_bq", "c_bk", "c_bv", "c_bo", "ff_b2",
                          "ln1_g", "ln1_b", "ln2_g", "ln2_b", "ln3_g", "ln3_b",
                          "norm1", "norm2", "bq", "bk", "bv", "bz", "bgz", "bgh", "bg2", "bgc2",
                          "abq", "abk", "abv", "abo", "bf2", "trans_b")]
VECS += [("ff_b1", FF // P), ("bf1", FF // P), ("bg1", 1), ("bgc1", 1)]
DERIVED = [(n, DC) for n in ("d_sq", "d_sk", "d_sv", "d_so", "d_cq", "d_ck", "d_cv", "d_co", "d_q2", "d_gz", "d_o2")]
DERIVED += [("d_k2", 1)]


def offsets(parts):
    at, out = 0, {}
    for name, size in parts:
        out[name] = at
        at += size
    return out, at


VAT, NVEC = offsets(VECS + DERIVED)
NVEC_IN = sum(s for _, s in VECS)
SQ = DC * D
W0 = [("so", SQ), ("co", SQ), ("ff1", DC * FF), ("ff2", FF // P * D)]
W0F = [("sq", SQ), ("sk", SQ), ("sv", SQ), ("cq", SQ), ("ck", SQ), ("cv", SQ), ("q2", SQ), ("k2", DC * 64)]
W1 = [("l1_sq", SQ), ("l1_sk", SQ), ("l1_sv", SQ), ("l1_so", SQ), ("g1", DC * FF), ("u1", DC * FF), ("d1", FF // P * D),
      ("l1_cq", SQ), ("l1_ck", SQ), ("l1_cv", SQ), ("l1_co", SQ), ("g2", DC * FF), ("u2", DC * FF), ("d2", FF // P * D)]
W2 = [("z", SQ), ("gz", SQ), ("v2", SQ), ("awk", SQ), ("awv", SQ), ("awo", SQ), ("wg1", DC * 64), ("wg2", D), ("gc2", D)]
WAT, NW = offsets(W0F + W0 + W1 + W2)
NWF = sum(s for _, s in W0F)
NW0, NW1, NW2 = (sum(s for _, s in w) for w in (W0, W1, W2))
FOLD_SRC = 2 * SQ
NSRC = len(FOLDS) * FOLD_SRC + SQ + DC * 64
NSRC_A = 6 * FOLD_SRC
T_W = [("wgh", SQ), ("f1", DC * FF), ("f2", FF // P * D), ("trans", 2 * SQ)]
NTW = sum(s for _, s in T_W)
TAT, NT = offsets(T_W + [("zs", DC * B * S), ("gzs", DC * B * S), ("gms", DC * B * S), ("base", DC * B * S), ("hs", DC * B * S)])
assert NT <= NW
CONSTS = [("ident", P), ("negid", P), ("neg", S), ("negT", S), ("hm16", 8), ("hm64", 2), ("hm32", 4), ("em4", 4), ("em2", 2)]
CAT, NCONST = offsets(CONSTS)


def constants():
    c = np.zeros((P, NCONST), np.float32)
    p = np.arange(P)
    c[p, CAT["ident"] + p] = 1.0
    c[p, CAT["negid"] + p] = -1.0
    q = np.arange(S)
    c[:S, CAT["neg"]:CAT["neg"] + S] = np.where(q[:, None] >= q[None, :], 0.0, MASKED)
    c[:S, CAT["negT"]:CAT["negT"] + S] = np.where(q[None, :] >= q[:, None], 0.0, MASKED)
    for name, rows in (("hm16", 16), ("hm64", 64), ("hm32", 32)):
        c[p, CAT[name] + p // rows] = 1.0
    c[p, CAT["em4"] + p % 64 // 16] = 1.0
    c[p, CAT["em2"] + p % 64 // 32] = 1.0
    return c


class Book:

    def __init__(self, known=None):
        self.marks = {}
        self.totals = {}
        self.banks = {}
        self.known = known


PHASES = [("prepare", 1), ("group", NG), ("load", 1), ("scan", S // 2), ("tail", NG)]


def build(nc, book, x_in, ctx_in, vec_in, const_in, src_in, w0_in, w1_in, w2_in, tw_in, out, spill):
    known = book.known
    with ExitStack() as ctx:
        def sb(name, shape, dt=F32):
            return ctx.enter_context(nc.sbuf_tensor(name, shape, dt))

        WT = sb("weights", [P, NW])
        X = sb("x_resid", [P, DC, N])
        T1 = sb("t1", [P, DC, N])
        T2 = sb("t2", [P, DC, N])
        QO = sb("q_then_o", [P, DC, N])
        K2 = sb("k_self", [P, DC, N])
        CT = sb("ctx_t", [P, GB, DC, C])
        KC = sb("k_ctx", [P, 2, DC, C])
        VA = sb("v_and_ones", [P, 2, 3, 6, 64])
        PQ = sb("probs_and_q", [P, 3 * 1200 + 3200])
        QBH = sb("q_blocks_bf", [P, 2, DC, 8 * S], BF16)
        KHB = sb("k_ctx_bf", [P, 2, DC, C], BF16)
        K2H = sb("k_self_bf", [P, DC, N], BF16)
        MD = sb("max_diag", [S, 2, 4, S], F32R)
        CST = sb("ctx_stage", [P, 3, D])
        EX = sb("extract", [P, 4, S])
        EM = sb("extract_m", [P, 4 * S])
        DN = sb("denoms", [P, DC, S])
        MX = sb("maxima", [S, 2, 16])
        VEC = sb("vectors", [P, NVEC])
        CO = sb("constants", [P, NCONST])
        ONEM = sb("ones_mean", [P, P])
        ONER = sb("ones_r", [S, P], F32R)
        IDB = sb("ident_bf", [S, S], BF16)
        NEGB = sb("neg_bf", [S, 4, S], BF16)
        NEGTB = sb("negT_bf", [S, 4, S], BF16)
        EPS = sb("eps", [P, 2])
        PS = ctx.enter_context(nc.psum_tensor("psum", [P, 8, 512], F32))

        state = [EM[:, i * DC * B:(i + 1) * DC * B].rearrange("p (c b) -> p c b", c=DC) for i in range(4)]
        GA, ZH, HG, GU = state
        HC = EX[:, 0, 0:2 * DC * B].rearrange("p (a c b) -> p a c b", a=2, c=DC)

        WP = QBH[:, :, :, :].rearrange("p a c n -> p (a c n)")[:, 0:3 * SQ].rearrange("p (r k d) -> p r k d", r=3, k=DC)
        HP = KHB[:, :, :, :].rearrange("p a c n -> p (a c n)")[:, 0:6 * DC * B].rearrange("p (a r c b) -> p a r c b", a=2, r=3, c=DC)
        HR = EX[:, 1, 0:DC * B].rearrange("p (c b) -> p c b", c=DC)
        WR = T1[:, :, 0:D]

        CTF = CT[:, :, :, :].rearrange("p b c k -> p (b c k)")
        PT = PQ[:, 0:3600].rearrange("p (r c n) -> p r c n", r=3, c=3)
        PF = PQ[:, 0:3600]
        QB = PQ[:, 3600:6800].rearrange("p (a c n) -> p a c n", a=2, c=DC)
        XST = PQ[:, 0:GB * D].rearrange("p (b d) -> p b d", b=GB)
        H = PQ[:, 0:3200].rearrange("p (m n) -> p m n", m=8)
        U = PQ[:, 3200:4000].rearrange("p (m n) -> p m n", m=2)
        GZ = PF[:, 0:800].rearrange("p (m n) -> p m n", m=2)
        GM = PF[:, 800:1600].rearrange("p (m n) -> p m n", m=2)
        GH = PF[:, 1600:2400].rearrange("p (m n) -> p m n", m=2)
        SG = PF[:, 2400:3200].rearrange("p (m n) -> p m n", m=2)
        PT3 = PF[:, 0:2 * 3 * S].rearrange("p (r c n) -> p r c n", r=2, c=3)
        PL3 = PF[:, 600:600 + 2 * C].rearrange("p (r n) -> p r n", r=2)
        YO = KC[:, :, :, :].rearrange("p r c n -> p (r c n)")[:, 0:GB * D].rearrange("p (b d) -> p b d", b=GB)
        CS3 = PQ[:, 3600:3600 + GB * 3 * D].rearrange("p (b c d) -> p b c d", b=GB, c=3)

        def w(name, k, m0, m1, width=D, rows=P):
            o = WAT[name] + k * width
            return WT[0:rows, o + m0:o + m1]

        def tw(name, k, m0, m1, width=D):
            o = TAT[name] + k * width
            return WT[:, o + m0:o + m1]

        def vec(name, m=0, rows=P):
            return VEC[0:rows, VAT[name] + m:VAT[name] + m + 1]

        def const(name, size, rows=P):
            return CO[0:rows, CAT[name]:CAT[name] + size]

        IDENT = const("ident", P)
        seq = lambda name: WT[:, TAT[name]:TAT[name] + DC * B * S]

        def sem(name):
            return ctx.enter_context(nc.semaphore(name))

        products_ready, act_results, dve_results, pool_results = (
            sem(n) for n in ("products_ready", "act_results", "dve_results", "pool_results"))
        x_loaded, ctx_loaded, weights_loaded, weights1_loaded, fold_sources_loaded = (
            sem(n) for n in ("x_loaded", "ctx_loaded", "weights_loaded", "weights1_loaded", "fold_sources_loaded"))
        constants_loaded, spilled, sequences_loaded, outputs_stored = (
            sem(n) for n in ("constants_loaded", "spilled", "sequences_loaded", "outputs_stored"))
        sems = {"pe": products_ready, "act": act_results, "dve": dve_results, "pool": pool_results, "x": x_loaded,
                "ctx": ctx_loaded, "w": weights_loaded, "w1": weights1_loaded, "src": fold_sources_loaded,
                "cst": constants_loaded, "spill": spilled, "seq": sequences_loaded, "out": outputs_stored}
        counts = dict.fromkeys(sems, 0)
        phase = {"name": None, "it": 0}
        waited = {}

        def before(track):
            total = 0
            for name, times in PHASES:
                per = known.totals.get((name, track), 0) if known else 0
                if name == phase["name"]:
                    return total, per
                total += per * times
            raise KeyError(phase["name"])

        def mark(track, point, by=1):
            counts[track] += by
            book.marks[phase["name"], point] = (track, counts[track])
            book.totals[phase["name"], track] = counts[track]
            return by

        def at(point):
            if not known:
                return 0
            track, n = known.marks[phase["name"], point]
            base, per = before(track)
            return phase["it"] * per + (base + n) if phase["loop"] else base + n

        def last(point):
            return at(point) - before(known.marks[phase["name"], point][0])[1] if known else 0

        def due(point):
            if not known:
                return True
            track, n = known.marks[phase["name"], point]
            if waited.get(track, 0) >= n:
                return False
            waited[track] = n
            return True

        def producer(point):
            return sems[known.marks[phase["name"], point][0]] if known else products_ready

        def enter(eng, name, it, of=None):
            phase.update(name=name, it=it, loop=dict(PHASES)[name] > 1)
            counts.update(dict.fromkeys(sems, 0))
            waited.clear()
            for track in (of or sems) if known else ():
                base, per = before(track)
                if phase["loop"] and per:
                    eng.wait_ge(sems[track], it * per + base)
                elif base:
                    eng.wait_ge(sems[track], base)

        def bank(use):
            return known.banks[phase["name"], use] if known else 0

        class Ring:

            def __init__(self, banks):
                self.banks = banks

            def start(self):
                self.k, self.freed = 0, {}

            def take(self, pe, use, freed_by):
                b = self.banks[self.k % len(self.banks)]
                self.k += 1
                if b in self.freed:
                    if due(self.freed[b]):
                        pe.wait_ge(producer(self.freed[b]), at(self.freed[b]))
                self.freed[b] = freed_by
                book.banks[phase["name"], use] = b
                return b

        rings = {"lin": Ring([0, 1]), "max": Ring([2, 3]), "st": Ring([4, 5]), "pv": Ring([6, 7])}

        def rings_start():
            for r in rings.values():
                r.start()

        ATT = {
            "s0": dict(heads=16, self=True, causal=True, mask="hm16", em="em4"),
            "c0": dict(heads=16, self=False, causal=False, mask="hm16", em="em4"),
            "s1": dict(heads=4, self=True, causal=False, mask="hm64", em=None),
            "c1": dict(heads=4, self=False, causal=False, mask="hm64", em=None),
            "c2": dict(heads=8, self=False, causal=False, mask="hm32", em="em2"),
        }
        for a in ATT.values():
            a["hc"] = a["heads"] // DC
            a["hg"] = a["heads"] // 4
            a["keys"] = SCH if a["self"] else KCH
            a["nu"] = a["heads"] // 4

        def groups_of(a, u):
            return range(4 * u // a["hg"], 4 * (u + 1) // a["hg"])

        WN = {"s0": ("sq", "sk", "sv"), "c0": ("cq", "ck", "cv"), "s1": ("l1_sq", "l1_sk", "l1_sv"),
              "c1": ("l1_cq", "l1_ck", "l1_cv"), "c2": ("q2", "awk", "awv")}
        QSC = {"s0": 1 / 16, "c0": 1 / 16, "s1": 1 / 8, "c1": 1 / 8, "c2": 1 / math.sqrt(32)}
        QBIAS = {"s0": "d_sq", "c0": "d_cq", "c2": "d_q2"}
        KBIAS = {"s0": "d_sk", "c0": "d_ck", "c2": "abk"}

        def keys_of(t, b, c, k0, kn):
            return K2[:, c, b * S + k0:b * S + k0 + kn] if ATT[t]["self"] else KC[:, b % 2, c, k0:k0 + kn]

        def qblock(b, c, h0, nh, hc):
            return QB[:, b % 2, c, h0 * S:(h0 + nh) * S]

        def pe_linear(pe, use, lhs, rhs, n, ms=DC, rows=P, ring="lin"):
            for m in range(ms):
                bk = rings[ring].take(pe, f"{use}{m}", f"{use}{m} out")
                for k, r in enumerate(rhs):
                    i = nc.tensor.matmul(PS[0:rows, bk, 0:n], lhs(k, m), r, start=k == 0, stop=k == len(rhs) - 1)
                i.then_inc(products_ready, mark("pe", f"{use}{m}"))

        def sq(name, rows=P):
            return lambda k, m: w(name, k, m * P, (m + 1) * P)

        def chunks(t):
            return [t[:, c, :] for c in range(DC)]

        def pe_kv(pe, t, b):
            if not ATT[t]["self"]:
                pe_keys(pe, t, b)
            pe_vals(pe, t, b)

        def pe_keys(pe, t, b):
            if due(f"ct{b} 1 out"):
                pe.wait_ge(act_results, at(f"ct{b} 1 out"))
            pe_linear(pe, f"{t} k{b} ", sq(WN[t][1]), [CT[:, b, c, :] for c in range(DC)], C)

        def pe_vals(pe, t, b):
            a = ATT[t]
            wv = WN[t][2]
            for kc, (k0, kn) in enumerate(a["keys"]):
                bk = rings["lin"].take(pe, f"{t} v{b} {kc}", f"{t} v{b} {kc} out")
                for c in range(DC):
                    lhs = X[:, c, b * S:(b + 1) * S] if a["self"] else CT[:, b, c, k0:k0 + kn]
                    i = nc.tensor.matmul(PS[0:kn, bk, 0:D], lhs, w(wv, c, 0, D), start=c == 0, stop=c == DC - 1)
                i.then_inc(products_ready, mark("pe", f"{t} v{b} {kc}"))

        def pe_max(pe, t, b, u, half=None):
            a = ATT[t]
            if due(f"{t} qh{b} 1"):
                pe.wait_ge(pool_results, at(f"{t} qh{b} 1"))
            if not a["self"]:
                if due(f"{t} kh{b} 1"):
                    pe.wait_ge(act_results, at(f"{t} kh{b} 1"))
            if a["self"]:
                bk = rings["max"].take(pe, f"{t} s{b} {u}", f"{t} m{b} {u}")
                for j in range(4):
                    c, hh = divmod(4 * u + j, a["hc"])
                    if a["causal"]:
                        nc.tensor.matmul(PS[0:S, bk, j * S:(j + 1) * S], IDB[:, :], NEGB[:, j, :], start=True, stop=False)
                    i = nc.tensor.matmul(PS[0:S, bk, j * S:(j + 1) * S], QBH[:, b % 2, c, hh * S:(hh + 1) * S],
                                         K2H[:, c, b * S:(b + 1) * S], start=not a["causal"], stop=True)
                i.then_inc(products_ready, mark("pe", f"{t} s{b} {u}"))
                return
            for h in range(4 * u + (2 if half == 1 else 0), 4 * u + (2 if half == 0 else 4)):
                c, hh = divmod(h, a["hc"])
                bk = rings["max"].take(pe, f"{t} s{b} {h}", f"{t} m{b} {h}")
                nc.tensor.matmul(PS[0:S, bk, 0:C], QBH[:, b % 2, c, hh * S:(hh + 1) * S], KHB[:, b % 2, c, :],
                                 start=True, stop=True).then_inc(products_ready, mark("pe", f"{t} s{b} {h}"))

        def pe_scores(pe, t, b, u):
            a = ATT[t]
            if due(f"{t} qb{b} 1"):
                pe.wait_ge(pool_results, at(f"{t} qb{b} 1"))
            if due(f"{t} md{b} {u}"):
                pe.wait_ge(dve_results, at(f"{t} md{b} {u}"))
            for kc, (k0, kn) in enumerate(a["keys"]):
                bk = rings["st"].take(pe, f"{t} st{b} {u} {kc}", f"{t} p{b} {u} {kc}")
                o = PS[0:kn, bk, :]
                nh = min(4, a["hc"])
                for j in range(0, 4, nh):
                    nc.tensor.matmul(o[:, j * S:(j + nh) * S], ONER[:, 0:kn], MD[:, (b * a["nu"] + u) % 2, j:j + nh, :], start=True, stop=False)
                    if a["causal"]:
                        nc.tensor.matmul(o[:, 0:N], IDB[:, :], NEGTB[:, :, :], start=False, stop=False)
                    c, hh = divmod(4 * u + j, a["hc"])
                    i = nc.tensor.matmul(o[:, j * S:(j + nh) * S], keys_of(t, b, c, k0, kn), qblock(b, c, hh, nh, a["hc"]),
                                         start=False, stop=True)
                i.then_inc(products_ready, mark("pe", f"{t} st{b} {u} {kc}"))

        def values_and_ones(b, kc, kn, g):
            first = 3 * (g // 2) + g % 2
            return VA[0:kn, b % 2, kc, first:first + 2, :]

        def pe_values(pe, t, b, u):
            a = ATT[t]
            hg = a["hg"]
            last = len(a["keys"]) - 1
            if due(f"{t} v{b} {last} out"):
                pe.wait_ge(act_results, at(f"{t} v{b} {last} out"))
            if due(f"{t} p{b} {u} {last}"):
                pe.wait_ge(act_results, at(f"{t} p{b} {u} {last}"))
            for g in groups_of(a, u):
                bk = rings["pv"].take(pe, f"{t} o{b} {g}", f"{t} e{b} {g}")
                for kc, (k0, kn) in enumerate(a["keys"]):
                    h0 = g * hg - 4 * u
                    i = nc.tensor.matmul(PS[:, bk, 0:hg * S], values_and_ones(b, kc, kn, g),
                                         PT[0:kn, (b * a["nu"] + u) % 3, kc, h0 * S:(h0 + hg) * S], start=kc == 0, stop=kc == last)
                i.then_inc(products_ready, mark("pe", f"{t} o{b} {g}"))

        def pe_attention(pe, t, src, ready, early=0, between=None):
            a = ATT[t]
            nu = a["nu"]
            for c in range(DC):
                if due(f"{ready}{c}"):
                    pe.wait_ge(producer(f"{ready}{c}"), at(f"{ready}{c}"))
            pe_linear(pe, f"{t} q ", sq(WN[t][0]), chunks(src), N)
            if a["self"]:
                pe_linear(pe, f"{t} k ", sq(WN[t][1]), chunks(src), N)
            for b in range(early, 2):
                pe_kv(pe, t, b)
            if a["self"]:
                if due(f"{t} kh 1"):
                    pe.wait_ge(act_results, at(f"{t} kh 1"))
            for u in range(nu):
                pe_max(pe, t, 0, u)
            for b in range(GB):
                for u in range(nu):
                    pe_scores(pe, t, b, u)
                    halves = (None,) if a["self"] else (0, 1)
                    kv = u == 0 and 1 <= b < GB - 1
                    if kv and not a["self"]:
                        pe_keys(pe, t, b + 1)
                    if b + 1 < GB:
                        pe_max(pe, t, b + 1, u, halves[0])
                    if kv:
                        pe_vals(pe, t, b + 1)
                    if u == 0 and between:
                        between(b)
                    if u:
                        pe_values(pe, t, b, u - 1)
                    if b + 1 < GB and len(halves) == 2:
                        pe_max(pe, t, b + 1, u, 1)
                pe_values(pe, t, b, nu - 1)

        def pe_norm(pe, t, mean=True, between=None):
            if mean:
                for c in range(DC):
                    if due(f"{t} y{c}"):
                        pe.wait_ge(dve_results, at(f"{t} y{c}"))
                pe_linear(pe, f"{t} mu ", lambda k, m: ONEM[:, :], chunks(T1), N, ms=1)
                if between:
                    between()
            for c in range(DC):
                if due(f"{t} sq{c}"):
                    pe.wait_ge(act_results, at(f"{t} sq{c}"))
            pe_linear(pe, f"{t} var ", lambda k, m: ONEM[:, :], chunks(T2), N, ms=1)

        def pe_down(pe, use, lhs, made="h{}"):
            for m in range(DC):
                bk = rings["lin"].take(pe, f"{use}{m}", f"{use}{m} out")
                for k in range(8):
                    if due(use + made.format(k)):
                        pe.wait_ge(producer(use + made.format(k)), at(use + made.format(k)))
                    i = nc.tensor.matmul(PS[:, bk, 0:N], lhs(k, m), H[:, k, :], start=k == 0, stop=k == 7)
                i.then_inc(products_ready, mark("pe", f"{use}{m}"))

        def pe_swiglu(pe, t, wg, wu, wd, ready):
            for c in range(DC):
                if due(f"{ready}{c}"):
                    pe.wait_ge(dve_results, at(f"{ready}{c}"))
            for m in range(8):
                for n, ww in (("g", wg), ("u", wu)):
                    bk = rings["lin" if n == "g" else "max"].take(pe, f"{t} {n}{m}", f"{t} {n}{m} out")
                    for k in range(DC):
                        i = nc.tensor.matmul(PS[:, bk, 0:N], w(ww, k, m * P, (m + 1) * P, FF), X[:, k, :], start=k == 0, stop=k == DC - 1)
                    i.then_inc(products_ready, mark("pe", f"{t} {n}{m}"))
            pe_down(pe, f"{t} ", lambda k, m: w(wd, k, m * P, (m + 1) * P))

        def pe_ctx(pe, b, staged, ring="lin"):
            if due(f"ctx{b}"):
                pe.wait_ge(ctx_loaded, at(f"ctx{b}"))
            for c in range(DC):
                bk = rings[ring].take(pe, f"ct{b} {c}", f"ct{b} {c} out")
                for kc, (k0, kn) in enumerate(KCH):
                    i = nc.tensor.transpose(PS[:, bk, k0:k0 + kn], staged[0:kn, kc, c * P:(c + 1) * P], IDENT[0:kn, 0:kn])
                i.then_inc(products_ready, mark("pe", f"ct{b} {c}"))

        def pe_gate_inputs(pe, point, t, s):
            for m in range(DC):
                o = TAT["gzs"] + m * B * S
                i = nc.tensor.matmul(PS[:, 2 * s + m, 0:B], IDENT, WT[:, o:o + (B + 1) * S][:, bass.ds(t, B, step=S)], start=True, stop=False)
            i.then_inc(products_ready, mark("pe", point))

        def pe_target_scores(pe, b):
            bk = rings["max"].take(pe, f"l3 s{b}", f"l3 p{b}")
            for c in range(DC):
                i = nc.tensor.matmul(PS[0:S, bk, 0:C], X[:, c, b * S:(b + 1) * S], CT[:, b, c, :], start=c == 0, stop=c == DC - 1)
            i.then_inc(products_ready, mark("pe", f"l3 s{b}"))

        def program_pe(pe):
            enter(pe, "prepare", 0)
            rings_start()
            if due("src"):
                pe.wait_ge(fold_sources_loaded, at("src"))
            if due("vectors"):
                pe.wait_ge(constants_loaded, at("vectors"))
            def src(o, k, width=D):
                o += k * width
                return PQ[:, o:o + width] if o < NSRC_A else CTF[:, o - NSRC_A:o - NSRC_A + width]

            for f, (name, b1, b2) in enumerate(FOLDS):
                o = f * FOLD_SRC
                for m in range(DC):
                    bk = rings["lin"].take(pe, f"fold {name}{m}", f"fold {name}{m} out")
                    for k in range(DC):
                        i = nc.tensor.matmul(PS[:, bk, 0:D], src(o, k)[:, m * P:(m + 1) * P], src(o + SQ, k), start=k == 0, stop=k == DC - 1)
                    i.then_inc(products_ready, mark("pe", f"fold {name}{m}"))
                    bk = rings["max"].take(pe, f"bias {name}{m}", f"bias {name}{m} out")
                    for k in range(DC):
                        i = nc.tensor.matmul(PS[:, bk, 0:1], src(o + SQ, k)[:, m * P:(m + 1) * P], vec(b1, k), start=k == 0, stop=k == DC - 1)
                    i.then_inc(products_ready, mark("pe", f"bias {name}{m}"))
            o = len(FOLDS) * FOLD_SRC
            for m in range(DC):
                bk = rings["lin"].take(pe, f"fold k2{m}", f"fold k2{m} out")
                for k in range(DC):
                    i = nc.tensor.matmul(PS[:, bk, 0:64], src(o, k)[:, m * P:(m + 1) * P], src(o + SQ, k, 64),
                                         start=k == 0, stop=k == DC - 1)
                i.then_inc(products_ready, mark("pe", f"fold k2{m}"))
            bk = rings["max"].take(pe, "bias k2", "bias k2 out")
            for k in range(DC):
                i = nc.tensor.matmul(PS[0:64, bk, 0:1], src(o + SQ, k, 64), vec("bk", k), start=k == 0, stop=k == DC - 1)
            i.then_inc(products_ready, mark("pe", "bias k2"))
            if due("w0"):
                pe.wait_ge(weights_loaded, at("w0"))
            if due("w2"):
                pe.wait_ge(weights_loaded, at("w2"))
            for name, ww, bv in (("so", "so", "d_sv"), ("co", "co", "d_cv"), ("o2", "awo", "abv")):
                if name != "o2":
                    if due(f"bias {bv[2:]}1 out"):
                        pe.wait_ge(dve_results, at(f"bias {bv[2:]}1 out"))
                for m in range(DC):
                    bk = rings["max"].take(pe, f"bias {name}{m}", f"bias {name}{m} out")
                    for k in range(DC):
                        i = nc.tensor.matmul(PS[:, bk, 0:1], w(ww, k, m * P, (m + 1) * P), vec(bv, k), start=k == 0, stop=k == DC - 1)
                    i.then_inc(products_ready, mark("pe", f"bias {name}{m}"))

            with pe.Fori(0, NG) as it:
                enter(pe, "group", it)
                rings_start()
                if due("x"):
                    pe.wait_ge(x_loaded, at("x"))
                for c in range(DC):
                    bk = rings["lin"].take(pe, f"xt {c}", f"xt {c} out")
                    for b in range(GB):
                        i = nc.tensor.transpose(PS[:, bk, b * S:(b + 1) * S], XST[0:S, b, c * P:(c + 1) * P], IDENT[0:S, 0:S])
                    i.then_inc(products_ready, mark("pe", f"xt {c}"))
                pe_attention(pe, "s0", X, "xr0 ", between=lambda b: pe_ctx(pe, b, CST))
                pe_kv(pe, "c0", 0)
                if due("s0 o done"):
                    pe.wait_ge(dve_results, at("s0 o done"))
                pe_linear(pe, "s0 w ", sq("so"), chunks(QO), N)
                pe_norm(pe, "n1", between=lambda: pe_kv(pe, "c0", 1))
                pe_attention(pe, "c0", X, "n1 x", early=2)
                if due("c0 o done"):
                    pe.wait_ge(dve_results, at("c0 o done"))
                pe_linear(pe, "c0 w ", sq("co"), chunks(QO), N)
                pe_norm(pe, "n2")
                for c in range(DC):
                    if due(f"n2 x{c}"):
                        pe.wait_ge(act_results, at(f"n2 x{c}"))
                for m in range(8):
                    bk = rings["lin"].take(pe, f"f0 h{m}", f"f0 h{m} out")
                    for k in range(DC):
                        i = nc.tensor.matmul(PS[:, bk, 0:N], w("ff1", k, m * P, (m + 1) * P, FF), X[:, k, :], start=k == 0, stop=k == DC - 1)
                    i.then_inc(products_ready, mark("pe", f"f0 h{m}"))
                pe_down(pe, "f0 ", lambda k, m: w("ff2", k, m * P, (m + 1) * P), "h{} out")
                pe_norm(pe, "n3")
                pe_attention(pe, "s1", X, "n3 x")
                pe_kv(pe, "c1", 0)
                if due("s1 o done"):
                    pe.wait_ge(dve_results, at("s1 o done"))
                pe_linear(pe, "s1 w ", sq("l1_so"), chunks(QO), N)
                pe_kv(pe, "c1", 1)
                pe_swiglu(pe, "f1", "g1", "u1", "d1", "s1 x")
                pe_attention(pe, "c1", X, "f1 x", early=2)
                pe_kv(pe, "c2", 0)
                if due("c1 o done"):
                    pe.wait_ge(dve_results, at("c1 o done"))
                pe_linear(pe, "c1 w ", sq("l1_co"), chunks(QO), N)
                pe_kv(pe, "c2", 1)
                pe_swiglu(pe, "f2", "g2", "u2", "d2", "c1 x")
                pe_norm(pe, "r1", mean=False)
                for c in range(DC):
                    if due(f"r1 x{c}"):
                        pe.wait_ge(dve_results, at(f"r1 x{c}"))
                pe_linear(pe, "z ", sq("z"), chunks(T1), N)
                for use, ww, src2 in (("ga ", "wg1", T2), ("gb ", "k2", T1)):
                    if use == "ga ":
                        if due("z 0 out"):
                            pe.wait_ge(act_results, at("z 0 out"))
                        if due("z 1 out"):
                            pe.wait_ge(act_results, at("z 1 out"))
                    bk = rings["lin"].take(pe, use, use + "out")
                    for k in range(DC):
                        o = WAT[ww] + k * 64
                        i = nc.tensor.matmul(PS[0:64, bk, 0:N], WT[:, o:o + 64], src2[:, k, :], start=k == 0, stop=k == DC - 1)
                    i.then_inc(products_ready, mark("pe", use))
                pe_linear(pe, "gz ", sq("gz"), chunks(T2), N)
                if due("ga out"):
                    pe.wait_ge(act_results, at("ga out"))
                pe_linear(pe, "gA ", lambda k, m: w("wg2", 0, m * P, (m + 1) * P, rows=64), [GH[0:64, 0, :]], N)
                if due("gb out"):
                    pe.wait_ge(act_results, at("gb out"))
                pe_linear(pe, "gB ", lambda k, m: w("gc2", 0, m * P, (m + 1) * P, rows=64), [GH[0:64, 1, :]], N)
                pe_attention(pe, "c2", T1, "r1 x", early=2)
                if due("c2 o done"):
                    pe.wait_ge(dve_results, at("c2 o done"))
                pe_linear(pe, "c2 w ", lambda k, m: w("awo" if k < DC else "v2", k % DC, m * P, (m + 1) * P), chunks(QO) + chunks(T1), N)

            enter(pe, "load", 0)
            rings_start()
            if due("ld base"):
                pe.wait_ge(sequences_loaded, at("ld base"))
            if due("h at rest"):
                pe.wait_ge(dve_results, at("h at rest"))
            pe_gate_inputs(pe, "first gz", 0, 0)
            with pe.Fori(0, S // 2) as it:
                phase.update(name="scan", it=it, loop=True)
                counts.update(dict.fromkeys(sems, 0))
                waited.clear()
                for s in range(2):
                    for part in range(3):
                        if s:
                            if due(f"hp0 {part}"):
                                pe.wait_ge(dve_results, at(f"hp0 {part}"))
                        else:
                            pe.wait_ge(dve_results, last(f"hp1 {part}"))
                        for m in range(DC):
                            for k in range(DC):
                                for wp in range(3):
                                    i = nc.tensor.matmul(PS[:, 2 * s + m, 0:B], WP[:, wp, k, m * P:(m + 1) * P], HP[:, s, part, k, :],
                                                         start=False, stop=part == wp == 2 and k == DC - 1)
                    i.then_inc(products_ready, mark("pe", f"gates{s}"))
                    if s:
                        if due("gate0"):
                            pe.wait_ge(act_results, at("gate0"))
                    else:
                        pe.wait_ge(act_results, last("gate1"))
                    pe_gate_inputs(pe, f"gz{s}", it * 2 + s + 1, 1 - s)
            for m in range(DC):
                nc.tensor.matmul(PS[:, m, 0:B], WP[:, 0, 0, 0:P], HP[:, 1, 0, 0, :], start=False, stop=True)

            with pe.Fori(0, NG) as it:
                enter(pe, "tail", it, [track for track in sems if track != "out"])
                rings_start()
                pe_norm(pe, "r2", mean=False)
                for c in range(DC):
                    if due(f"r2 x{c}"):
                        pe.wait_ge(dve_results, at(f"r2 x{c}"))
                for m in range(8):
                    bk = rings["lin"].take(pe, f"ft h{m}", f"ft h{m} out")
                    for k in range(DC):
                        i = nc.tensor.matmul(PS[:, bk, 0:N], tw("f1", k, m * P, (m + 1) * P, FF), T1[:, k, :], start=k == 0, stop=k == DC - 1)
                    i.then_inc(products_ready, mark("pe", f"ft h{m}"))
                if due(f"ctx{GB - 1}"):
                    pe.wait_ge(ctx_loaded, at(f"ctx{GB - 1}"))
                for b in range(GB):
                    pe_ctx(pe, b, CS3[:, b], ring="st")
                for m in range(DC):
                    bk = rings["lin"].take(pe, f"ft {m}", f"ft x{m}")
                    for k in range(8):
                        if due(f"ft h{k} out"):
                            pe.wait_ge(act_results, at(f"ft h{k} out"))
                        i = nc.tensor.matmul(PS[:, bk, 0:N], tw("f2", k, m * P, (m + 1) * P), H[:, k, :], start=k == 0, stop=k == 7)
                    i.then_inc(products_ready, mark("pe", f"ft {m}"))
                for c in range(DC):
                    if due(f"ct{GB - 1} {c} out"):
                        pe.wait_ge(act_results, at(f"ct{GB - 1} {c} out"))
                    if due(f"ft x{c}"):
                        pe.wait_ge(dve_results, at(f"ft x{c}"))
                for b in range(2):
                    pe_target_scores(pe, b)
                for b in range(GB):
                    if due(f"l3 pn{b}"):
                        pe.wait_ge(dve_results, at(f"l3 pn{b}"))
                    bk = rings["st"].take(pe, f"l3 pt{b}", f"l3 pt{b} out")
                    for kc, (k0, kn) in enumerate(KCH):
                        i = nc.tensor.transpose(PS[0:kn, bk, kc * S:(kc + 1) * S], PL3[0:S, b % 2, k0:k0 + kn], IDENT[0:S, 0:S])
                    i.then_inc(products_ready, mark("pe", f"l3 pt{b}"))
                    if b + 2 < GB:
                        pe_target_scores(pe, b + 2)
                    if due(f"l3 pt{b} out"):
                        pe.wait_ge(act_results, at(f"l3 pt{b} out"))
                    bk = rings["pv"].take(pe, f"l3 ti{b}", f"l3 ti{b} out")
                    for c in range(DC):
                        for kc, (k0, kn) in enumerate(KCH):
                            i = nc.tensor.matmul(PS[:, bk, c * S:(c + 1) * S], CS3[0:kn, b, kc, c * P:(c + 1) * P], PT3[0:kn, b % 2, kc, :],
                                                 start=kc == 0, stop=kc == 2)
                    i.then_inc(products_ready, mark("pe", f"l3 ti{b}"))
                for m in range(DC):
                    bk = rings["lin"].take(pe, f"l3 y {m}", f"l3 y {m} out")
                    for k, r in enumerate(chunks(X) + chunks(T1)):
                        if k == DC:
                            if due(f"l3 ti{GB - 1} out"):
                                pe.wait_ge(act_results, at(f"l3 ti{GB - 1} out"))
                        i = nc.tensor.matmul(PS[:, bk, 0:N], tw("trans", k, m * P, (m + 1) * P), r, start=k == 0, stop=k == 2 * DC - 1)
                    i.then_inc(products_ready, mark("pe", f"l3 y {m}"))
                for m in range(DC):
                    if due(f"l3 r{m}"):
                        pe.wait_ge(dve_results, at(f"l3 r{m}"))
                for b in range(GB):
                    bk = rings["max"].take(pe, f"l3 out{b}", f"l3 out{b} out")
                    for m in range(DC):
                        i = nc.tensor.transpose(PS[0:S, bk, m * P:(m + 1) * P], T2[:, m, b * S:(b + 1) * S], IDENT)
                    i.then_inc(products_ready, mark("pe", f"l3 out{b}"))

        def act_evac(act, use, out, func=ACT.Identity, rows=P, n=N, point=None, **kw):
            if due(use):
                act.wait_ge(products_ready, at(use))
            nc.scalar.activation(out, PS[0:rows, bank(use), 0:n], func, **kw).then_inc(act_results, mark("act", point or f"{use} out"))

        def act_kv(act, t, b):
            a = ATT[t]
            if not a["self"]:
                kw = [{"bias": vec(KBIAS[t], m)} if t in KBIAS else {} for m in range(DC)]
                for m in range(DC):
                    act_evac(act, f"{t} k{b} {m}", KHB[:, b % 2, m, :], n=C, point=f"{t} kh{b} {m}", **kw[m])
                    act_evac(act, f"{t} k{b} {m}", KC[:, b % 2, m, :], n=C, **kw[m])
            for kc, (k0, kn) in enumerate(a["keys"]):
                if due(f"{t} v{b} {kc}"):
                    act.wait_ge(products_ready, at(f"{t} v{b} {kc}"))
                src = PS[0:kn, bank(f"{t} v{b} {kc}"), 0:D].rearrange("p (c s i) -> p c s i", c=DC, s=2)
                dst = VA[0:kn, b % 2, kc, :, :].rearrange("p (c s) i -> p c s i", c=DC)[:, :, 0:3:2, :]
                nc.scalar.activation(dst, src, ACT.Copy).then_inc(act_results, mark("act", f"{t} v{b} {kc} out"))

        def act_attention(act, t, early=0, between=None):
            a = ATT[t]
            nu = a["nu"]
            last = len(a["keys"]) - 1
            for m in range(DC):
                kw = {"bias": vec(QBIAS[t], m)} if t in QBIAS else {}
                act_evac(act, f"{t} q {m}", QO[:, m, :], scale=QSC[t], **kw)
            if a["self"]:
                for m in range(DC):
                    kw = {"bias": vec(KBIAS[t], m)} if t in KBIAS else {}
                    act_evac(act, f"{t} k {m}", K2[:, m, :], point=f"{t} kf {m}", **kw)
                    act_evac(act, f"{t} k {m}", K2H[:, m, :], point=f"{t} kh {m}", **kw)
                    mark_same(f"{t} k {m} out", f"{t} kh {m}")
            for b in range(early, 2):
                act_kv(act, t, b)
            for b in range(GB):
                for u in range(nu):
                    i = b * nu + u
                    if i >= 3:
                        old = f"{t} o{(i - 3) // nu} {groups_of(a, (i - 3) % nu)[-1]}"
                        if due(old):
                            act.wait_ge(products_ready, at(old))
                    for kc, (k0, kn) in enumerate(a["keys"]):
                        if due(f"{t} st{b} {u} {kc}"):
                            act.wait_ge(products_ready, at(f"{t} st{b} {u} {kc}"))
                        nc.scalar.activation(PT[0:kn, i % 3, kc, :], PS[0:kn, bank(f"{t} st{b} {u} {kc}"), 0:N],
                                             ACT.Exp).then_inc(act_results, mark("act", f"{t} p{b} {u} {kc}"))
                    if u == 0 and 1 <= b < GB - 1:
                        if due(f"{t} o{b - 1} 3"):
                            act.wait_ge(products_ready, at(f"{t} o{b - 1} 3"))
                        act_kv(act, t, b + 1)
                    if u == 0 and between:
                        between(b)

        def act_norm(act, t, eps, gain=None, bias=None, mean=True, src=None):
            for c in range(DC):
                if due(f"{t} c{c}"):
                    act.wait_ge(dve_results, at(f"{t} c{c}"))
                nc.scalar.activation(T2[:, c, :], (T1 if mean else X)[:, c, :], ACT.Square).then_inc(act_results, mark("act", f"{t} sq{c}"))
            if due(f"{t} var 0"):
                act.wait_ge(products_ready, at(f"{t} var 0"))
            nc.scalar.activation(T2[:, 0, :], PS[:, bank(f"{t} var 0"), 0:N], ACT.Sqrt, bias=EPS[:, eps:eps + 1]).then_inc(act_results, mark("act", f"{t} var 0 out"))
            if gain:
                for c in range(DC):
                    if due(f"{t} t{c}"):
                        act.wait_ge(dve_results, at(f"{t} t{c}"))
                    nc.scalar.activation(X[:, c, :], T1[:, c, :], ACT.Identity, scale=vec(gain, c), bias=vec(bias, c)).then_inc(act_results, mark("act", f"{t} x{c}"))

        def act_swiglu(act, t):
            for m in range(8):
                if m >= 2:
                    if due(f"{t} h{m - 2}"):
                        act.wait_ge(dve_results, at(f"{t} h{m - 2}"))
                act_evac(act, f"{t} g{m}", U[:, m % 2, :], func=ACT.Silu)

        def act_ctx(act, b):
            for c in range(DC):
                act_evac(act, f"ct{b} {c}", CT[:, b, c, :], n=C, func=ACT.Copy)

        def act_target_probs(act, b):
            if due(f"l3 m{b}"):
                act.wait_ge(dve_results, at(f"l3 m{b}"))
            if b >= 2:
                if due(f"l3 pt{b - 2}"):
                    act.wait_ge(products_ready, at(f"l3 pt{b - 2}"))
            nc.scalar.activation(PL3[0:S, b % 2, :], PS[0:S, bank(f"l3 s{b}"), 0:C], ACT.Exp, bias=MX[:, b % 2, 0:1],
                                 accum_out=MX[:, b % 2, 1:2]).then_inc(act_results, mark("act", f"l3 p{b}"))

        def program_act(act):
            enter(act, "prepare", 0)
            for name, _, _ in FOLDS:
                for m in range(DC):
                    o = WAT[name] + m * D
                    act_evac(act, f"fold {name}{m}", WT[:, o:o + D], n=D, func=ACT.Copy)
            for m in range(DC):
                o = WAT["k2"] + m * 64
                act_evac(act, f"fold k2{m}", WT[:, o:o + 64], n=64, func=ACT.Copy)

            with act.Fori(0, NG) as it:
                enter(act, "group", it)
                for c in range(DC):
                    act_evac(act, f"xt {c}", X[:, c, :], func=ACT.Copy)
                    book.marks["group", f"xr0 {c}"] = book.marks["group", f"xt {c} out"]
                act_attention(act, "s0", between=lambda b: act_ctx(act, b))
                act_kv(act, "c0", 0)
                act_kv(act, "c0", 1)
                act_norm(act, "n1", 0, "ln1_g", "ln1_b")
                act_attention(act, "c0", early=2)
                act_norm(act, "n2", 0, "ln2_g", "ln2_b")
                for m in range(8):
                    act_evac(act, f"f0 h{m}", H[:, m, :], func=ACT.Gelu, bias=vec("ff_b1", m))
                act_norm(act, "n3", 0, "ln3_g", "ln3_b")
                act_attention(act, "s1")
                act_kv(act, "c1", 0)
                act_kv(act, "c1", 1)
                act_swiglu(act, "f1")
                act_attention(act, "c1", early=2)
                act_kv(act, "c2", 0)
                act_kv(act, "c2", 1)
                act_swiglu(act, "f2")
                act_norm(act, "r1", 1, mean=False)
                if due("r1 x1"):
                    act.wait_ge(dve_results, at("r1 x1"))
                for m in range(DC):
                    act_evac(act, f"z {m}", T2[:, m, :], bias=vec("bz", m))
                act_evac(act, "ga ", GH[0:64, 0, :], rows=64, func=ACT.Gelu_apprx_tanh, bias=vec("bg1", rows=64), point="ga out")
                act_evac(act, "gb ", GH[0:64, 1, :], rows=64, func=ACT.Gelu_apprx_tanh, bias=vec("d_k2", rows=64), point="gb out")
                for m in range(DC):
                    act_evac(act, f"gz {m}", GZ[:, m, :], bias=vec("d_gz", m))
                for m in range(DC):
                    act_evac(act, f"gA {m}", SG[:, m, :], func=ACT.Sigmoid, bias=vec("bg2", m))
                for m in range(DC):
                    act_evac(act, f"gB {m}", GM[:, m, :], func=ACT.Sigmoid, bias=vec("bgc2", m))
                if due("spill gm"):
                    act.wait_ge(spilled, at("spill gm"))
                act_attention(act, "c2", early=2)

            enter(act, "load", 0)
            with act.Fori(0, S // 2) as it:
                enter(act, "scan", it, ("pe",))
                for s in range(2):
                    if due(f"gates{s}"):
                        act.wait_ge(products_ready, at(f"gates{s}"))
                    nc.scalar.activation(GA[:, :, :], PS[:, 2 * s:2 * s + 2, 0:B], ACT.Sigmoid).then_inc(act_results, mark("act", f"gate{s}"))

            with act.Fori(0, NG) as it:
                enter(act, "tail", it, [track for track in sems if track != "out"])
                act_norm(act, "r2", 1, mean=False)
                for m in range(8):
                    act_evac(act, f"ft h{m}", H[:, m, :], func=ACT.Gelu_apprx_tanh, bias=vec("bf1", m))
                for b in range(GB):
                    act_ctx(act, b)
                for b in range(2):
                    act_target_probs(act, b)
                for b in range(GB):
                    if b >= 2:
                        if due(f"l3 ti{b - 2}"):
                            act.wait_ge(products_ready, at(f"l3 ti{b - 2}"))
                    for kc, (k0, kn) in enumerate(KCH):
                        if due(f"l3 pt{b}"):
                            act.wait_ge(products_ready, at(f"l3 pt{b}"))
                        i = nc.scalar.activation(PT3[0:kn, b % 2, kc, :], PS[0:kn, bank(f"l3 pt{b}"), kc * S:(kc + 1) * S], ACT.Copy)
                    i.then_inc(act_results, mark("act", f"l3 pt{b} out"))
                    if b + 2 < GB:
                        act_target_probs(act, b + 2)
                    if due(f"l3 ti{b}"):
                        act.wait_ge(products_ready, at(f"l3 ti{b}"))
                    src = PS[:, bank(f"l3 ti{b}"), 0:DC * S].rearrange("p (c n) -> p c n", c=DC)
                    nc.scalar.activation(T1[:, :, b * S:(b + 1) * S], src, ACT.Copy).then_inc(act_results, mark("act", f"l3 ti{b} out"))
                for m in range(DC):
                    act_evac(act, f"l3 y {m}", T2[:, m, :], func=ACT.Tanh, bias=vec("trans_b", m))
                base, per = before("out")
                act.wait_ge(outputs_stored, it * per + base)
                for b in range(GB):
                    act_evac(act, f"l3 out{b}", YO[0:S, b, :], rows=S, n=D, func=ACT.Copy)

        def dve_attention(dve, t):
            a = ATT[t]
            hg, heads = a["hg"], a["heads"]

            nu = a["nu"]

            def maxima(b, u):
                if b >= 2:
                    if due(f"{t} md{b - 2} {nu - 1}"):
                        dve.wait_ge(dve_results, at(f"{t} md{b - 2} {nu - 1}"))
                if a["self"]:
                    if due(f"{t} s{b} {u}"):
                        dve.wait_ge(products_ready, at(f"{t} s{b} {u}"))
                    src = PS[0:S, bank(f"{t} s{b} {u}"), 0:N].rearrange("p (h k) -> p h k", h=4)
                    nc.vector.reduce_max(MX[:, b % 2, 4 * u:4 * u + 4], src, AX).then_inc(dve_results, mark("dve", f"{t} m{b} {u}"))
                    return
                for h in range(4 * u, 4 * u + 4):
                    if due(f"{t} s{b} {h}"):
                        dve.wait_ge(products_ready, at(f"{t} s{b} {h}"))
                    nc.vector.reduce_max(MX[:, b % 2, h:h + 1], PS[0:S, bank(f"{t} s{b} {h}"), 0:C],
                                         AX).then_inc(dve_results, mark("dve", f"{t} m{b} {h}"))

            def diagonals(i):
                b, u = divmod(i, nu)
                if i >= 2:
                    old = f"{t} st{(i - 2) // nu} {(i - 2) % nu} {len(a['keys']) - 1}"
                    if due(old):
                        dve.wait_ge(products_ready, at(old))
                top = f"{t} m{b} {u if a['self'] else 4 * u + 3}"
                if due(top):
                    dve.wait_ge(dve_results, at(top))
                nc.vector.tensor_tensor(MD[:, i % 2, :, :], const("negid", S, S).unsqueeze(1).broadcast_to([S, 4, S]),
                                        MX[:, b % 2, 4 * u:4 * u + 4].unsqueeze(2).broadcast_to([S, 4, S]),
                                        ALU.mult).then_inc(dve_results, mark("dve", f"{t} md{b} {u}"))

            def outputs(b, u):
                for g in groups_of(a, u):
                    if due(f"{t} o{b} {g}"):
                        dve.wait_ge(products_ready, at(f"{t} o{b} {g}"))
                    src = PS[:, bank(f"{t} o{b} {g}"), 0:hg * S].rearrange("p (h q) -> p h q", h=hg)
                    if b or g:
                        old = f"{t} x{b if g else b - 1} {g - 1 if g else 3}"
                        if due(old):
                            dve.wait_ge(dve_results, at(old))
                    if hg == 1:
                        nc.vector.tensor_copy(EX[:, g, :], src[:, 0, :]).then_inc(dve_results, mark("dve", f"{t} e{b} {g}"))
                        mark_same(f"{t} x{b} {g}", f"{t} e{b} {g}")
                        continue
                    em = EM[:, 0:hg * S].rearrange("p (h q) -> p h q", h=hg)
                    msk = const(a["em"], hg).unsqueeze(2).broadcast_to([P, hg, S])
                    nc.vector.tensor_tensor(em, src, msk, ALU.mult).then_inc(dve_results, mark("dve", f"{t} e{b} {g}"))
                    if due(f"{t} e{b} {g}"):
                        dve.wait_ge(dve_results, at(f"{t} e{b} {g}"))
                    nc.vector.reduce_sum(EX[:, g, :], em.rearrange("p h q -> p q h"), AX).then_inc(dve_results, mark("dve", f"{t} x{b} {g}"))

            def normalise(b):
                if due(f"{t} x{b} 3"):
                    dve.wait_ge(dve_results, at(f"{t} x{b} 3"))
                nc.vector.tensor_copy(DN[0:64, :, :], EX[64:128, 0:4:2, :]).then_inc(dve_results, mark("dve", f"{t} dn{b} 0"))
                nc.vector.tensor_copy(DN[64:128, :, :], EX[0:64, 1:4:2, :]).then_inc(dve_results, mark("dve", f"{t} dn{b} 1"))
                if due(f"{t} dn{b} 1"):
                    dve.wait_ge(dve_results, at(f"{t} dn{b} 1"))
                nc.vector.reciprocal(DN[:, :, :], DN[:, :, :]).then_inc(dve_results, mark("dve", f"{t} rc{b}"))
                if due(f"{t} rc{b}"):
                    dve.wait_ge(dve_results, at(f"{t} rc{b}"))
                if due(f"{t} qb{b} 1"):
                    dve.wait_ge(pool_results, at(f"{t} qb{b} 1"))
                o = QO[:, :, b * S:(b + 1) * S]
                done = f"{t} o done" if b == GB - 1 else f"{t} oo{b} 1"
                nc.vector.tensor_tensor(o[0:64], EX[0:64, 0:4:2, :], DN[0:64, :, :], ALU.mult).then_inc(dve_results, mark("dve", f"{t} oo{b} 0"))
                nc.vector.tensor_tensor(o[64:128], EX[64:128, 1:4:2, :], DN[64:128, :, :], ALU.mult).then_inc(dve_results, mark("dve", done))
                if due(done):
                    dve.wait_ge(dve_results, at(done))

            for u in range(nu):
                maxima(0, u)
            diagonals(0)
            for b in range(GB):
                for u in range(nu):
                    if b * nu + u + 1 < GB * nu and nu > 1:
                        diagonals(b * nu + u + 1)
                    if b + 1 < GB:
                        maxima(b + 1, u)
                        if nu == 1:
                            diagonals(b + 1)
                    if u:
                        outputs(b, u - 1)
                outputs(b, nu - 1)
                normalise(b)

        def mark_same(new, old):
            book.marks[phase["name"], new] = book.marks[phase["name"], old]

        def dve_residual(dve, use, out, bias, point, resid):
            for m in range(DC):
                if due(f"{use}{m}"):
                    dve.wait_ge(products_ready, at(f"{use}{m}"))
                pin = PS[:, bank(f"{use}{m}"), 0:N]
                if bias:
                    i = nc.vector.scalar_tensor_tensor(out[:, m, :], pin, vec(bias, m), resid[:, m, :], ALU.add, ALU.add)
                else:
                    i = nc.vector.tensor_tensor(out[:, m, :], pin, resid[:, m, :], ALU.add)
                i.then_inc(dve_results, mark("dve", f"{point}{m}"))
                mark_same(f"{use}{m} out", f"{point}{m}")

        def dve_center(dve, t):
            if due(f"{t} mu 0"):
                dve.wait_ge(products_ready, at(f"{t} mu 0"))
            for c in range(DC):
                if due(f"{t} y{c}"):
                    dve.wait_ge(dve_results, at(f"{t} y{c}"))
                nc.vector.tensor_tensor(T1[:, c, :], T1[:, c, :], PS[:, bank(f"{t} mu 0"), 0:N], ALU.subtract).then_inc(dve_results, mark("dve", f"{t} c{c}"))
            mark_same(f"{t} mu 0 out", f"{t} c1")
            dve_scale(dve, t)

        def dve_scale(dve, t, gain=None):
            if due(f"{t} var 0 out"):
                dve.wait_ge(act_results, at(f"{t} var 0 out"))
            nc.vector.reciprocal(T2[:, 0, :], T2[:, 0, :]).then_inc(dve_results, mark("dve", f"{t} rs"))
            if due(f"{t} rs"):
                dve.wait_ge(dve_results, at(f"{t} rs"))
            for c in range(DC):
                if gain:
                    nc.vector.scalar_tensor_tensor(T1[:, c, :], X[:, c, :], vec(gain, c), T2[:, 0, :], ALU.mult, ALU.mult).then_inc(dve_results, mark("dve", f"{t} x{c}"))
                else:
                    nc.vector.tensor_tensor(T1[:, c, :], T1[:, c, :], T2[:, 0, :], ALU.mult).then_inc(dve_results, mark("dve", f"{t} t{c}"))

        def dve_swiglu(dve, t):
            for m in range(8):
                if due(f"{t} g{m} out"):
                    dve.wait_ge(act_results, at(f"{t} g{m} out"))
                if due(f"{t} u{m}"):
                    dve.wait_ge(products_ready, at(f"{t} u{m}"))
                nc.vector.tensor_tensor(H[:, m, :], PS[:, bank(f"{t} u{m}"), 0:N], U[:, m % 2, :], ALU.mult).then_inc(dve_results, mark("dve", f"{t} h{m}"))
                mark_same(f"{t} u{m} out", f"{t} h{m}")

        def dve_target_max(dve, b):
            if due(f"l3 s{b}"):
                dve.wait_ge(products_ready, at(f"l3 s{b}"))
            if b >= 2:
                if due(f"l3 pn{b - 2}"):
                    dve.wait_ge(dve_results, at(f"l3 pn{b - 2}"))
            nc.vector.tensor_reduce(MX[:, b % 2, 0:1], PS[0:S, bank(f"l3 s{b}"), 0:C], AX, ALU.max, negate=True).then_inc(dve_results, mark("dve", f"l3 m{b}"))

        def program_dve(dve):
            enter(dve, "prepare", 0)
            if due("constants"):
                dve.wait_ge(constants_loaded, at("constants"))
            nc.vector.memset(ONEM[:, :], 1.0 / D).then_inc(dve_results, mark("dve", "p0"))
            nc.vector.memset(VA[:, :, :, 1:6:3, :], 1.0).then_inc(dve_results, mark("dve", "p1"))
            nc.vector.memset(EPS[:, 0:1], 1e-5).then_inc(dve_results, mark("dve", "p2"))
            nc.vector.memset(EPS[:, 1:2], 1e-6).then_inc(dve_results, mark("dve", "p3"))
            nc.vector.memset(EM[:, 0:P], 1.0).then_inc(dve_results, mark("dve", "p4"))
            if due("p4"):
                dve.wait_ge(dve_results, at("p4"))
            nc.vector.tensor_copy(ONER[:, :], EM[0:S, 0:P]).then_inc(dve_results, mark("dve", "p6"))
            nc.vector.tensor_copy(IDB[:, :], const("ident", S, S)).then_inc(dve_results, mark("dve", "p7"))
            nc.vector.tensor_copy(NEGB[:, :, :], const("neg", S, S).unsqueeze(1).broadcast_to([S, 4, S])).then_inc(dve_results, mark("dve", "p8"))
            nc.vector.tensor_copy(NEGTB[:, :, :], const("negT", S, S).unsqueeze(1).broadcast_to([S, 4, S])).then_inc(dve_results, mark("dve", "p9"))
            if due("vectors"):
                dve.wait_ge(constants_loaded, at("vectors"))
            for name, _, b2 in FOLDS:
                scale = {"sq": 1 / 16, "cq": 1 / 16, "q2": 1 / math.sqrt(32)}.get(name, 1.0)
                for m in range(DC):
                    if due(f"bias {name}{m}"):
                        dve.wait_ge(products_ready, at(f"bias {name}{m}"))
                    nc.vector.tensor_scalar(vec(f"d_{name}", m), PS[:, bank(f"bias {name}{m}"), 0:1], vec(b2, m), scale, ALU.add, ALU.mult).then_inc(dve_results, mark("dve", f"bias {name}{m} out"))
            if due("bias k2"):
                dve.wait_ge(products_ready, at("bias k2"))
            nc.vector.tensor_scalar(vec("d_k2", rows=64), PS[0:64, bank("bias k2"), 0:1], vec("bgc1", rows=64), None, ALU.add).then_inc(dve_results, mark("dve", "bias k2 out"))
            nc.vector.tensor_tensor(VEC[:, VAT["d_gz"]:VAT["d_gz"] + 2], VEC[:, VAT["bgz"]:VAT["bgz"] + 2],
                                        VEC[:, VAT["bgh"]:VAT["bgh"] + 2], ALU.add).then_inc(dve_results, mark("dve", "d_gz"))
            for name, b2 in (("so", "m_bo"), ("co", "c_bo"), ("o2", "abo")):
                for m in range(DC):
                    if due(f"bias {name}{m}"):
                        dve.wait_ge(products_ready, at(f"bias {name}{m}"))
                    nc.vector.tensor_scalar(vec(f"d_{name}", m), PS[:, bank(f"bias {name}{m}"), 0:1], vec(b2, m), None, ALU.add).then_inc(dve_results, mark("dve", f"bias {name}{m} out"))
            if due("bias o21 out"):
                dve.wait_ge(dve_results, at("bias o21 out"))
            for m in range(DC):
                nc.vector.scalar_tensor_tensor(vec("d_o2", m), vec("bv", m), 0.1, vec("d_o2", m), ALU.mult, ALU.add).then_inc(dve_results, mark("dve", f"dd{m}"))
            if due("w2"):
                dve.wait_ge(weights_loaded, at("w2"))
            o = WAT["v2"]
            nc.vector.tensor_scalar(WT[:, o:o + SQ], WT[:, o:o + SQ], 0.1, None, ALU.mult).then_inc(dve_results, mark("dve", "v2"))

            with dve.Fori(0, NG) as it:
                enter(dve, "group", it)
                dve_attention(dve, "s0")
                dve_residual(dve, "s0 w ", T1, "d_so", "n1 y", X)
                dve_center(dve, "n1")
                dve_attention(dve, "c0")
                dve_residual(dve, "c0 w ", T1, "d_co", "n2 y", X)
                dve_center(dve, "n2")
                dve_residual(dve, "f0 ", T1, "ff_b2", "n3 y", X)
                dve_center(dve, "n3")
                dve_attention(dve, "s1")
                dve_residual(dve, "s1 w ", X, None, "s1 x", X)
                dve_swiglu(dve, "f1")
                dve_residual(dve, "f1 ", X, None, "f1 x", X)
                dve_attention(dve, "c1")
                dve_residual(dve, "c1 w ", X, None, "c1 x", X)
                dve_swiglu(dve, "f2")
                dve_residual(dve, "f2 ", X, None, "r1 c", X)
                dve_scale(dve, "r1", gain="norm1")
                for m in range(DC):
                    if due(f"gB {m} out"):
                        dve.wait_ge(act_results, at(f"gB {m} out"))
                    nc.vector.tensor_tensor(GM[:, m, :], GM[:, m, :], SG[:, m, :], ALU.mult).then_inc(dve_results, mark("dve", f"gm a{m}"))
                    if due(f"gm a{m}"):
                        dve.wait_ge(dve_results, at(f"gm a{m}"))
                    nc.vector.tensor_scalar(GM[:, m, :], GM[:, m, :], 1e-6, 1.0 - 1e-6, ALU.max, ALU.min).then_inc(dve_results, mark("dve", f"gm b{m}"))
                    if due(f"gm b{m}"):
                        dve.wait_ge(dve_results, at(f"gm b{m}"))
                    nc.vector.tensor_scalar(GM[:, m, :], GM[:, m, :], 1.0, None, ALU.add).then_inc(dve_results, mark("dve", f"gm{m}"))
                dve_attention(dve, "c2")
                dve_residual(dve, "c2 w ", X, "d_o2", "base", X)

            enter(dve, "load", 0)
            nc.vector.memset(HC[:, 0, :, :], 0.0).then_inc(dve_results, mark("dve", "h0 at rest"))
            if due("ld base"):
                dve.wait_ge(sequences_loaded, at("ld base"))
            o = TAT["wgh"]
            wgh = WT[:, o:o + SQ].rearrange("p (k d) -> p k d", k=DC)
            nc.vector.tensor_copy(WP[:, 0], wgh).then_inc(dve_results, mark("dve", "wp0"))
            if due("wp0"):
                dve.wait_ge(dve_results, at("wp0"))
            nc.vector.tensor_tensor(WR, wgh, WP[:, 0], ALU.subtract).then_inc(dve_results, mark("dve", "wr"))
            if due("wr"):
                dve.wait_ge(dve_results, at("wr"))
            nc.vector.tensor_copy(WP[:, 1], WR).then_inc(dve_results, mark("dve", "wp1"))
            if due("wp1"):
                dve.wait_ge(dve_results, at("wp1"))
            nc.vector.tensor_tensor(WP[:, 2], WR, WP[:, 1], ALU.subtract).then_inc(dve_results, mark("dve", "wp2"))
            nc.vector.memset(HP[:, 0], 0.0).then_inc(dve_results, mark("dve", "h at rest"))

            def steps(name, t):
                return seq(name).rearrange("p (c b t) -> p c b t", c=DC, b=B)[:, :, :, bass.ds(t, 1)]

            with dve.Fori(0, S // 2) as it:
                enter(dve, "scan", it, ("act", "dve", "pool"))
                for s in range(2):
                    h = HC[:, s, :, :].unsqueeze(3)
                    t = it * 2 + s
                    if s:
                        if due("h0"):
                            dve.wait_ge(dve_results, at("h0"))
                    nc.vector.tensor_tensor(ZH[:, :, :].unsqueeze(3), steps("zs", t), h, ALU.subtract).then_inc(dve_results, mark("dve", f"zh{s}"))
                    nc.vector.tensor_tensor(HG[:, :, :].unsqueeze(3), steps("gms", t), h, ALU.mult).then_inc(dve_results, mark("dve", f"hg{s}"))
                    if due(f"gate{s}"):
                        dve.wait_ge(act_results, at(f"gate{s}"))
                    if due(f"hg{s}"):
                        dve.wait_ge(dve_results, at(f"hg{s}"))
                    nc.vector.tensor_tensor(GU[:, :, :], GA[:, :, :], ZH[:, :, :], ALU.mult).then_inc(dve_results, mark("dve", f"gu{s}"))
                    if due(f"gu{s}"):
                        dve.wait_ge(dve_results, at(f"gu{s}"))
                    nc.vector.tensor_tensor(HP[:, 1 - s, 0], GU[:, :, :], HG[:, :, :], ALU.add).then_inc(dve_results, mark("dve", f"hp{s} 0"))
                    nc.vector.tensor_tensor(HC[:, 1 - s, :, :], GU[:, :, :], HG[:, :, :], ALU.add).then_inc(dve_results, mark("dve", f"h{s}"))
                    if due(f"h{s}"):
                        dve.wait_ge(dve_results, at(f"h{s}"))
                    nc.vector.tensor_tensor(HP[:, 1 - s, 1], HC[:, 1 - s, :, :], HP[:, 1 - s, 0], ALU.subtract).then_inc(dve_results, mark("dve", f"hp{s} 1"))
                    nc.vector.tensor_tensor(HR, HC[:, 1 - s, :, :], HP[:, 1 - s, 0], ALU.subtract).then_inc(dve_results, mark("dve", f"hr{s}"))
                    if due(f"hr{s}"):
                        dve.wait_ge(dve_results, at(f"hr{s}"))
                    nc.vector.tensor_tensor(HP[:, 1 - s, 2], HR, HP[:, 1 - s, 1], ALU.subtract).then_inc(dve_results, mark("dve", f"hp{s} 2"))

            with dve.Fori(0, NG) as it:
                enter(dve, "tail", it, [track for track in sems if track != "out"])
                for c in range(DC):
                    o = lambda name: seq(name)[:, bass.ds(it * N + c * B * S, N)]
                    nc.vector.tensor_tensor(X[:, c, :], o("base"), o("hs"), ALU.add).then_inc(dve_results, mark("dve", f"r2 c{c}"))
                dve_scale(dve, "r2", gain="norm2")
                dve_residual(dve, "ft ", X, "bf2", "ft x", X)
                dve_target_max(dve, 0)
                for b in range(GB):
                    if b + 1 < GB:
                        dve_target_max(dve, b + 1)
                    if due(f"l3 p{b}"):
                        dve.wait_ge(act_results, at(f"l3 p{b}"))
                    nc.vector.reciprocal(MX[:, b % 2, 1:2], MX[:, b % 2, 1:2]).then_inc(dve_results, mark("dve", f"l3 rc{b}"))
                    if due(f"l3 rc{b}"):
                        dve.wait_ge(dve_results, at(f"l3 rc{b}"))
                    nc.vector.tensor_scalar(PL3[0:S, b % 2, :], PL3[0:S, b % 2, :], MX[:, b % 2, 1:2], None, ALU.mult).then_inc(dve_results, mark("dve", f"l3 pn{b}"))
                for m in range(DC):
                    if due(f"l3 y {m} out"):
                        dve.wait_ge(act_results, at(f"l3 y {m} out"))
                    nc.vector.tensor_tensor(T2[:, m, :], T2[:, m, :], X[:, m, :], ALU.add).then_inc(dve_results, mark("dve", f"l3 r{m}"))

        def program_pool(pool):
            enter(pool, "prepare", 0)
            nc.gpsimd.memset(QO[:, 0, 0:1], 0.0).then_inc(pool_results, mark("pool", "begun"))
            with pool.Fori(0, NG) as it:
                enter(pool, "group", it)
                for t in ("s0", "c0", "s1", "c1", "c2"):
                    a = ATT[t]
                    hc = a["hc"]
                    if due(f"{t} q 1 out"):
                        pool.wait_ge(act_results, at(f"{t} q 1 out"))
                    for b in range(GB):
                        if b >= 2:
                            old = f"{t} st{b - 2} {a['nu'] - 1} {len(a['keys']) - 1}"
                            if due(old):
                                pool.wait_ge(products_ready, at(old))
                        for to, name in ((QBH, "qh"), (QB, "qb")):
                            for c in range(DC):
                                nc.gpsimd.tensor_tensor(to[:, b % 2, c, 0:hc * S].rearrange("p (h q) -> p h q", h=hc),
                                                        QO[:, c, b * S:(b + 1) * S].unsqueeze(1).broadcast_to([P, hc, S]),
                                                        const(a["mask"], hc).unsqueeze(2).broadcast_to([P, hc, S]),
                                                        ALU.mult).then_inc(pool_results, mark("pool", f"{t} {name}{b} {c}"))
            enter(pool, "load", 0)
            with pool.Fori(0, S // 2) as it:
                enter(pool, "scan", it)
                for s in range(2):
                    if due(f"h{s}"):
                        pool.wait_ge(dve_results, at(f"h{s}"))
                    dst = seq("hs").rearrange("p (c b t) -> p c b t", c=DC, b=B)[:, :, :, bass.ds(it * 2 + s, 1)]
                    nc.gpsimd.tensor_copy(dst, HC[:, 1 - s, :, :].unsqueeze(3)).then_inc(pool_results, mark("pool", f"hs{s}"))

        def load_ctx(sp, row, b, staged, used=None):
            if used:
                if due(used):
                    sp.wait_ge(products_ready, at(used))
            for kc, (k0, kn) in enumerate(KCH):
                src = ctx_in[bass.ds(row, 1), k0:k0 + kn, :].rearrange("a k d -> (a k) d")
                sp.dma_start(staged[0:kn, kc, :], src).then_inc(ctx_loaded, mark("ctx", f"ctx{b}" if kc == 2 else f"ctx{b} {kc}", 16))

        def program_sp(sp):
            enter(sp, "prepare", 0)
            for track in ("x", "ctx", "spill", "out"):
                sp.sem_inc(sems[track], mark(track, f"{track} begun", 16))
            sp.dma_start(VEC[:, 0:NVEC_IN], vec_in).then_inc(constants_loaded, mark("cst", "vectors0", 16))
            sp.dma_start(CO[:, :], const_in).then_inc(constants_loaded, mark("cst", "constants", 16))
            mark_same("vectors", "constants")
            sp.dma_start(PQ[:, 0:NSRC_A], src_in[:, 0:NSRC_A]).then_inc(fold_sources_loaded, mark("src", "src a", 16))
            sp.dma_start(CTF[:, 0:NSRC - NSRC_A], src_in[:, NSRC_A:NSRC]).then_inc(fold_sources_loaded, mark("src", "src", 16))
            sp.dma_start(WT[:, NWF:NWF + NW0], w0_in).then_inc(weights_loaded, mark("w", "w0a", 16))
            sp.dma_start(WT[:, NWF + NW0 + NW1:NW], w2_in).then_inc(weights_loaded, mark("w", "w2", 16))
            mark_same("w0", "w2")
            sp.dma_start(WT[:, NWF + NW0:NWF + NW0 + NW1], w1_in).then_inc(weights1_loaded, mark("w1", "w1", 16))
            with sp.Fori(0, NG) as it:
                rows_at = [sp.snap(it * GB + b) for b in range(GB)]
                col_at = sp.snap(it * N)
                enter(sp, "group", it, ("pe", "act", "dve"))
                sp.dma_start(XST[0:S, :, :], x_in[bass.ds(rows_at[0], GB), :, :].rearrange("b s d -> s b d")).then_inc(x_loaded, mark("x", "x", 16))
                for b in range(GB):
                    load_ctx(sp, rows_at[b], b, CST, f"ct{b - 1} 1" if b else None)
                for k, (name, t, points) in enumerate((("z", T2, ("z 1 out",)), ("gz", GZ, ("gz 1 out",)), ("gm", GM, ("gm1",)), ("base", X, ("base1",)))):
                    for p in points:
                        if due(p):
                            sp.wait_ge(producer(p), at(p))
                    sp.dma_start(spill[k, :, :, bass.ds(col_at, N)], t[:, :, :]).then_inc(spilled, mark("spill", f"spill {name}", 16))
            enter(sp, "load", 0)
            sp.dma_start(WT[:, 0:NTW], tw_in).then_inc(sequences_loaded, mark("seq", "tw", 16))
            for k, name in enumerate(("zs", "gzs", "gms", "base")):
                sp.dma_start(seq(name).rearrange("p (c n) -> p c n", c=DC), spill[k]).then_inc(sequences_loaded, mark("seq", f"ld {name}", 16))
            with sp.Fori(0, NG) as it:
                rows_at = [sp.snap(it * GB + b) for b in range(GB)]
                enter(sp, "tail", it, ("pe",))
                for b in range(GB):
                    load_ctx(sp, rows_at[b], b, CS3[:, b])
                if due(f"l3 out{GB - 1} out"):
                    sp.wait_ge(act_results, at(f"l3 out{GB - 1} out"))
                sp.dma_start(out[bass.ds(rows_at[0], GB), :, :].rearrange("b s d -> s b d"), YO[0:S, :, :]).then_inc(outputs_stored, mark("out", "out", 16))
            if known:
                sp.wait_ge(outputs_stored, NG * 16 + 16)

        block = ctx.enter_context(nc.Block())

        @block.sync
        def _(sp):
            program_sp(sp)

        @block.scalar
        def _(act):
            program_act(act)

        @block.vector
        def _(dve):
            program_dve(dve)

        @block.gpsimd
        def _(pool):
            program_pool(pool)

        @block.tensor
        def _(pe):
            program_pe(pe)


def rows(a):
    k, m = a.shape
    return a.reshape(k // P, P, m).transpose(1, 0, 2).reshape(P, -1)


def column(v):
    if v.size < P:
        v = np.concatenate([v, np.zeros(P - v.size, v.dtype)])
    return v.reshape(-1, P).T


def kernel(**inputs):
    import concourse.bacc as bacc
    from concourse.bass_utils import run_bass_kernel_spmd as run

    i0 = {k[9:]: np.asarray(v) for k, v in inputs.items() if k.startswith("L0_")}
    i1 = {k[9:]: np.asarray(v) for k, v in inputs.items() if k.startswith("L1_")}
    i2 = {k[9:]: np.asarray(v) for k, v in inputs.items() if k.startswith("L2_")}
    i3 = {k[9:]: np.asarray(v) for k, v in inputs.items() if k.startswith("L3_")}
    cat = lambda parts: np.ascontiguousarray(np.concatenate(parts, axis=1))
    vals = dict(i0)
    vals.update({"norm1": i2["norm1_scale"], "norm2": i2["norm2_scale"], "trans_b": i3["trans_b"]})
    for n in ("bq", "bk", "bv", "bz", "bgz", "bgh", "bg2", "bgc2", "abq", "abk", "abv", "abo", "bf2", "bf1", "bg1", "bgc1"):
        vals[n] = i2[n]
    heads = lambda a: a.reshape(D, D).T
    pad64 = lambda a: np.concatenate([a, np.zeros((P - a.shape[0], a.shape[1]), a.dtype)])
    src = []
    for a, b in (("sa_q_W", "m_Wq"), ("sa_k_W", "m_Wk"), ("sa_v_W", "m_Wv"), ("ca_q_W", "c_Wq"), ("ca_k_W", "c_Wk"), ("ca_v_W", "c_Wv")):
        src += [rows(i0[a]), rows(heads(i0[b]))]
    src += [rows(i2["Wq"].T), rows(i2["Awq"]), rows(i2["Wk"].T), rows(i2["Wgc1"])]
    arrays = {
        "x": np.asarray(inputs["x"]), "ctx": np.asarray(inputs["ctx_1024"]),
        "vec": cat([column(vals[n].reshape(-1)) for n, _ in VECS]),
        "const": constants(),
        "src": cat(src),
        "w0": cat([rows(i0["m_Wo"].T), rows(i0["c_Wo"].T), rows(i0["ff_W1"].T), rows(i0["ff_W2"].T)]),
        "w1": cat([rows(i1[n]) for n in ("sa_wq", "sa_wk", "sa_wv", "sa_wo", "samlp_wg", "samlp_wu", "samlp_wd",
                                         "ca_wq", "ca_wk", "ca_wv", "ca_wo", "camlp_wg", "camlp_wu", "camlp_wd")]),
        "w2": cat([rows(i2[n]) for n in ("Wz", "Wgz", "Wv", "Awk", "Awv", "Awo", "Wg1")] + [pad64(i2["Wg2"]), pad64(i2["Wgc2"])]),
        "tw": cat([rows(i2["Wgh"]), rows(i2["Wf1"]), rows(i2["Wf2"]), rows(i3["trans_W"])]),
    }

    def make(book):
        nc = bacc.Bacc("TRN2", target_bir_lowering=False, num_devices=1)
        ins = [nc.dram_tensor(f"in_{n}", a.shape, mybir.dt.from_np(a.dtype), kind="ExternalInput").ap() for n, a in arrays.items()]
        out = nc.dram_tensor("out", (B, S, D), F32, kind="ExternalOutput").ap()
        spill = nc.dram_tensor("spill", (4, P, DC, B * S), F32, kind="Internal").ap()
        build(nc, book, *ins, out, spill)
        return nc

    counted = Book()
    make(counted)
    nc = make(Book(counted))
    r = run(nc, [{f"in_{n}": a for n, a in arrays.items()}], core_ids=[0])
    return r.results[0]["out"]
```
